# Optimizing a Trainium2 kernel written in Bass

```python
import numpy as np
import jax
import jax.numpy as jnp

def _softmax(x, axis=-1):
    return jax.nn.softmax(x, axis=axis)

def _gelu(x):
    return jax.nn.gelu(x, approximate=True)

def _silu(x):
    return jax.nn.silu(x)

def _sigmoid(x):
    return jax.nn.sigmoid(x)

def _layernorm(x, axis=-1, eps=1e-05):
    m = jnp.mean(x, axis=axis, keepdims=True)
    v = jnp.var(x, axis=axis, keepdims=True)
    return (x - m) / jnp.sqrt(v + eps)

def _scatter_add(tgt, idx, src, axis=0):
    return tgt.at[idx].add(src)

def _segment_sum(src, seg, n):
    return jax.ops.segment_sum(src, seg, n)
kernel_name = 'mk_gnn_resnorm_d2_gnn_r8_6564ee'

def setup_inputs(seed: int=0):
    np.random.seed(seed)
    _w = jnp.asarray

    def _rec_inputs():
        import jax
        import jax.numpy as jnp
        _gk = jax.random.key(seed)
        x = -0.000202 + 1 * jax.random.normal(jax.random.fold_in(_gk, 1), (12500, 256), jnp.float32)
        src = jax.random.randint(jax.random.fold_in(_gk, 2), (200000,), 0, 12500, jnp.int32)
        dst = jax.random.randint(jax.random.fold_in(_gk, 3), (200000,), 0, 12500, jnp.int32)
        _o = jnp.argsort(dst, stable=True)
        src = src[_o]
        dst = dst[_o]
        return (x, src, dst)
    x, src, dst = _rec_inputs()

    def _L0_gnn_setup():
        import jax, jax.numpy as jnp
        import numpy as np
        N_NODES = 3125
        N_EDGES = 50000
        D = 256
        key = jax.random.key(seed)
        k1, k2, k3, k4, k5 = jax.random.split(key, 5)
        feat = jax.random.normal(k1, (N_NODES, D), dtype=jnp.float32)
        src = jax.random.randint(k2, (N_EDGES,), 0, N_NODES, dtype=jnp.int32)
        dst = jax.random.randint(k3, (N_EDGES,), 0, N_NODES, dtype=jnp.int32)
        a = float(np.sqrt(6.0 / (D + D)))
        W1 = jax.random.uniform(k4, (D, D), minval=-a, maxval=a, dtype=jnp.float32)
        W2 = jax.random.uniform(k5, (D, D), minval=-a, maxval=a, dtype=jnp.float32)
        b = jnp.zeros((D,), dtype=jnp.float32)
        return {'feat': feat, 'W1': W1, 'W2': W2, 'b': b, 'src': src, 'dst': dst}
    _L0_gnn_all = _L0_gnn_setup()
    _L0_gnn_in = {k: v for k, v in _L0_gnn_all.items() if k in ('W1', 'W2', 'b')}
    del _L0_gnn_all

    def _L1_gnn_setup():
        import jax, jax.numpy as jnp
        import numpy as np
        N_NODES = 12500
        N_EDGES = 200000
        IN_DIM = 256
        OUT_DIM = 256
        key = jax.random.key(seed)
        k1, k2, k3 = jax.random.split(key, 3)
        x = jax.random.normal(k1, (N_NODES, IN_DIM), dtype=jnp.float32)
        limit = 0.1 * np.sqrt(6.0 / (IN_DIM + OUT_DIM))
        W = jax.random.uniform(k2, (OUT_DIM, IN_DIM), dtype=jnp.float32, minval=-limit, maxval=limit)
        b = jnp.zeros((OUT_DIM,), dtype=jnp.float32)
        edge_index = jax.random.randint(k3, (2, N_EDGES), 0, N_NODES, dtype=jnp.int64)
        return {'x': x, 'W': W, 'b': b, 'edge_index': edge_index}
    _L1_gnn_all = _L1_gnn_setup()
    _L1_gnn_in = {k: v for k, v in _L1_gnn_all.items() if k in ('W', 'b')}
    del _L1_gnn_all
    return {'x': x, 'src': src, 'dst': dst, 'L0_gnn_W1': _L0_gnn_in['W1'], 'L0_gnn_W2': _L0_gnn_in['W2'], 'L0_gnn_b': _L0_gnn_in['b'], 'L1_gnn_W': _L1_gnn_in['W'], 'L1_gnn_b': _L1_gnn_in['b']}

def reference(x, src, dst, L0_gnn_W1, L0_gnn_W2, L0_gnn_b, L1_gnn_W, L1_gnn_b):
    import jax
    import jax.numpy as jnp

    def _L0_gnn_ref(feat, W1, W2, b, src, dst):
        import jax, jax.numpy as jnp
        import numpy as np
        N_NODES = 3125
        N_EDGES = 50000
        D = 256
        n = feat.shape[0]
        ones = jnp.ones(src.shape[0], dtype=feat.dtype)
        out_deg = jnp.maximum(jax.ops.segment_sum(ones, src, num_segments=n), 1.0)
        in_cnt = jax.ops.segment_sum(ones, dst, num_segments=n)
        t1 = feat @ W1
        msg = t1[src] + feat[src] * feat[dst] @ W2
        scale = jnp.sqrt(out_deg[src]) * jnp.sqrt(out_deg[dst])
        msg = msg / scale[:, None]
        agg = jax.ops.segment_sum(msg, dst, num_segments=n)
        embed = jnp.where(in_cnt[:, None] > 0, t1 + agg, jnp.zeros_like(t1))
        embed = embed + b
        embed = jax.nn.leaky_relu(embed, negative_slope=0.01)
        norm = jnp.linalg.norm(embed, axis=1, keepdims=True)
        embed = embed / jnp.maximum(norm, 1e-12)
        return embed

    def _L1_gnn_ref(x, W, b, edge_index):
        import jax, jax.numpy as jnp
        import numpy as np
        N_NODES = 12500
        N_EDGES = 200000
        IN_DIM = 256
        OUT_DIM = 256
        num_nodes = x.shape[0]
        src, tgt = (edge_index[0], edge_index[1])
        xt = jnp.einsum('ni,oi->no', x, W) + b
        out = jax.ops.segment_sum(xt[src], tgt, num_segments=num_nodes)
        deg = jax.ops.segment_sum(jnp.ones_like(tgt, dtype=x.dtype), tgt, num_segments=num_nodes)
        out = out / (deg + 1.0)[:, None]
        return out
    edge_index = jnp.stack([src, dst])
    x = _layernorm(x + _L0_gnn_ref(x, L0_gnn_W1, L0_gnn_W2, L0_gnn_b, src, dst), axis=-1)
    x = _layernorm(x + _L1_gnn_ref(x, L1_gnn_W, L1_gnn_b, edge_index), axis=-1)
    return x

_drawn_inputs = setup_inputs


def setup_inputs(seed=0):
    import zlib

    import numpy as np

    out = dict(_drawn_inputs(seed))
    spreads = {'L0_gnn_b': (0.0, 0.8), 'L1_gnn_b': (0.0, 0.1)}
    factors = {'L0_gnn_W2': 3.893}
    for name, (base, spread) in spreads.items():
        noise = np.random.default_rng([zlib.crc32(name.encode()), seed]).standard_normal(out[name].shape)
        drawn = base * np.exp(spread * noise) if base else spread * noise
        out[name] = jnp.asarray(drawn.astype(out[name].dtype))
    for name, factor in factors.items():
        out[name] = (out[name] * factor).astype(out[name].dtype)
    return out
```

```python
import concourse.bass as bass
from concourse import mybir
from contextlib import ExitStack

F32, BF16, I32 = mybir.dt.float32, mybir.dt.bfloat16, mybir.dt.int32
ALU = mybir.AluOpType
ACT = mybir.ActivationFunctionType
AX = mybir.AxisListType

P = 128
D = 256
KF = D // P
NODES = 12500
EDGES = 200000
NW = -(-NODES // P)
NPAD = NW * P
LAST_ROWS = NODES - (NW - 1) * P
ROUNDS = NW // 2
U = 32
TILES = ROUNDS * U
GT = 4
GR = U // GT
GROUPS = TILES // GT
WIN = 64
ACC_N = NPAD + WIN
BLOCKS = -(-TILES // P)
FULL_TILES = EDGES // P
LAST_EDGES = EDGES - FULL_TILES * P
LAST_BLOCK_TILES = TILES - (BLOCKS - 1) * P
PAD_SRC = NPAD - 1
PAD_DST = NODES
HB = 16
HBATCHES = TILES // HB
HI = NW
QT = U // 4
XCH = 14
DUMP = NPAD


def gnn(nc, x, src, dst, w1, w2, b0, wl, b1, out):
    table = [nc.dram_tensor("scaled_x", (NPAD, D), F32, kind="Internal").ap(),
             nc.dram_tensor("x1", (NPAD, D), F32, kind="Internal").ap()]
    base_dram = nc.dram_tensor("group_bases", (BLOCKS * U,), I32, kind="Internal").ap()
    sums_dram = [nc.dram_tensor(f"sums{n}", (NPAD + P, D), F32, kind="Internal").ap() for n in range(2)]

    with ExitStack() as ctx:
        def sb(name, shape, dt=F32):
            return ctx.enter_context(nc.sbuf_tensor(name, shape, dt))

        def sem(name):
            return ctx.enter_context(nc.semaphore(name))

        big = sb("big", [P, KF * ACC_N])
        acc = big[:, :].rearrange("p (k n) -> p k n", k=KF)
        x_all = big[:, 0:NW * D].rearrange("p (w f) -> p w f", w=NW)
        ring = sb("ring", [P, U, D])
        ring_flat = ring[:, :, :].rearrange("p u f -> p (u f)")
        nat = [ring_flat[:, n * BLOCKS * P:(n + 1) * BLOCKS * P] for n in range(2)]
        nat_i = [ring_flat[:, (2 + n) * BLOCKS * P:(3 + n) * BLOCKS * P].bitcast(I32) for n in range(2)]
        src_col = sb("src_col", [P, TILES + U], I32)
        digit_t = sb("digit_t", [P, TILES], I32)
        dst_col = sb("dst_col", [P, TILES])
        dst_rel = sb("dst_rel", [P, TILES + GT])
        src_digits = ring_flat[:, 2 * BLOCKS * P:3 * BLOCKS * P].bitcast(BF16)
        lo = [src_digits[:, 0:TILES], sb("dst_lo", [P, TILES], BF16)[:, :]]
        hi = [src_digits[:, TILES:2 * TILES], sb("dst_hi", [P, TILES], BF16)[:, :]]
        count_to = sb("count_to", [P, P, HB], BF16)
        lo_hot = [sb(f"lo_hot{n}", [P, P, HB], BF16) for n in range(2)]
        hi_hot = [sb(f"hi_hot{n}", [P, HI, HB], BF16) for n in range(2)]
        win_iota = sb("win_iota", [P, WIN])
        dst_hot = sb("dst_hot", [P, 2, GT, WIN])
        idx = sb("idx", [P, U], I32)
        ident = sb("ident", [P, P])
        lower = sb("lower", [P, P])
        ones = sb("ones", [P, P])
        zeros = sb("zeros", [P, D])
        dump_row = sb("dump_row", [P, 1])
        epsilon = sb("epsilon", [P, 1])
        bounds = sb("bounds", [P, 2, BLOCKS])
        gmin = sb("gmin", [BLOCKS, U])
        gmax = sb("gmax", [BLOCKS, U])
        floor_i = sb("floor_i", [BLOCKS, U], I32)
        floor_f = sb("floor_f", [BLOCKS, U])
        gmin_i = sb("gmin_i", [BLOCKS, U], I32)
        bad = sb("bad", [BLOCKS, 4])
        flag = sb("flag", [1, 1], I32)
        base_row = sb("base_row", [1, BLOCKS * U], I32)
        base_row_f = dst_hot[0:1, :, :, :].rearrange("p a b c -> p (a b c)")[:, 0:BLOCKS * U]
        r = sb("r", [P, NW])
        deg = sb("deg", [P, NW])
        w1_s = sb("w1_s", [P, KF, D])
        w2_s = sb("w2_s", [P, KF, D])
        wt_s = sb("wt_s", [P, KF, D])
        b0_s = sb("b0_s", [P, D])
        b1_s = sb("b1_s", [P, D])
        x_t = [sb(f"x_t{n}", [P, D]) for n in range(2)]
        a_t = [sb(f"a_t{n}", [P, KF, P]) for n in range(2)]
        out_t = [sb(f"out_t{n}", [P, D]) for n in range(2)]
        sums_t = sb("sums_t", [P, D])
        xT = sb("xT", [P, KF, P])
        xa = sb("xa", [P, KF, P])
        xw = sb("xw", [P, D])
        e = sb("e", [P, D])
        h = sb("h", [P, D])
        scal = sb("scal", [P, 8])
        stats = sb("stats", [P, 6])
        mv = sb("mv", [P, 2])

        banks = ctx.enter_context(nc.psum_tensor("banks", [P, 8, 512], F32))

        def group_sum(buf):
            return banks[:, 2 * buf:2 * buf + 2, 0:WIN]

        def hist(half):
            return banks[:, 4 + half, 0:HI]

        consts_made = sem("consts_made")
        edges_loaded = sem("edges_loaded")
        edges_padded = sem("edges_padded")
        weights_loaded = sem("weights_loaded")
        x_loaded = sem("x_loaded")
        x_padded = sem("x_padded")
        edges_float = sem("edges_float")
        edges_turned = sem("edges_turned")
        edges_in_cols = sem("edges_in_cols")
        bounds_made = sem("bounds_made")
        bounds_turned = sem("bounds_turned")
        bad_counted = sem("bad_counted")
        bad_summed = sem("bad_summed")
        bases_made = sem("bases_made")
        bases_stored = sem("bases_stored")
        bases_loaded = sem("bases_loaded")
        bases_float = sem("bases_float")
        bases_spread = sem("bases_spread")
        flag_made = sem("flag_made")
        w_turned = sem("w_turned")
        w_copied = sem("w_copied")
        hot_made = sem("hot_made")
        hot_used = sem("hot_used")
        degree_ready = sem("degree_ready")
        degree_rooted = sem("degree_rooted")
        r_made = sem("r_made")
        x_scaled_act = sem("x_scaled_act")
        x_scaled = sem("x_scaled")
        table_stored = [sem(f"table_stored{c}") for c in range(NW // XCH)]
        acc_zeroed = sem("acc_zeroed")
        idx_ready = sem("idx_ready")
        rows_in = [sem(f"rows_in{u}") for u in range(U)]
        gather_turn = sem("gather_turn")
        dst_hot_made = sem("dst_hot_made")
        tiles_done = sem("tiles_done")
        groups_added = sem("groups_added")
        act_turn = sem("act_turn")
        x_in = [sem(f"x_in{n}") for n in range(2)]
        sums_in = sem("sums_in")
        stored = [sem(f"stored{n}") for n in range(2)]
        node_done = [sem(f"node_done{n}") for n in range(2)]
        out_ready = [sem(f"out_ready{n}") for n in range(2)]
        a_ready = [sem(f"a_ready{n}") for n in range(2)]
        x_turned = sem("x_turned")
        sums_turned = sem("sums_turned")
        xT_ready = sem("xT_ready")
        xa_ready = sem("xa_ready")
        xw_done = sem("xw_done")
        xw_ready = sem("xw_ready")
        projected = sem("projected")
        square_ready = sem("square_ready")
        norm_ready = sem("norm_ready")
        var_ready = sem("var_ready")
        var_rooted = sem("var_rooted")
        table1_whole = sem("table1_whole")
        dcol_ready = sem("dcol_ready")
        drow_spread = sem("drow_spread")
        same_ready = sem("same_ready")
        to_ready = sem("to_ready")
        combined = sem("combined")
        comb_ready = sem("comb_ready")
        one_idx_ready = sem("one_idx_ready")
        row_in = sem("row_in")
        row_added = sem("row_added")
        sums_zeroed = sem("sums_zeroed")

        block = ctx.enter_context(nc.Block())

        def group_no(layer, i, k):
            return layer * GROUPS + i * GR + k

        def node_no(layer, m):
            return layer * ROUNDS + m

        @block.sync
        def _(sp):
            sp.wait_ge(edges_padded, 1)
            for n, edges in enumerate((src, dst)):
                whole = (BLOCKS - 1) * P
                v = nat_i[n].rearrange("p (b e) -> p b e", b=BLOCKS)
                sp.dma_start(v[:, 0:BLOCKS - 1, :],
                             edges[0:whole * P].rearrange("(b p e) -> p b e", p=P, e=P)).then_inc(edges_loaded, 16)
                sp.dma_start(v[0:FULL_TILES - whole, BLOCKS - 1, :],
                             edges[whole * P:FULL_TILES * P].rearrange("(p e) -> p e", e=P)).then_inc(edges_loaded, 16)
                sp.dma_start(v[FULL_TILES - whole:FULL_TILES - whole + 1, BLOCKS - 1, 0:LAST_EDGES],
                             edges[FULL_TILES * P:EDGES].rearrange("(p e) -> p e", p=1)).then_inc(edges_loaded, 16)
            sp.wait_ge(x_padded, 1)
            x_rows = x[0:(NW - 1) * P, :].rearrange("(w p) f -> p w f", p=P)
            sp.dma_start(x_all[:, 0:NW - 1, :], x_rows).then_inc(x_loaded, 16)
            sp.dma_start(x_all[0:LAST_ROWS, NW - 1, :], x[(NW - 1) * P:NODES, :]).then_inc(x_loaded, 16)
            sp.dma_start(w1_s[:, :, :], w1.rearrange("(k p) n -> p k n", p=P)).then_inc(weights_loaded, 16)
            sp.dma_start(w2_s[:, :, :], w2.rearrange("(k p) n -> p k n", p=P)).then_inc(weights_loaded, 16)
            sp.dma_start(xT[:, :, :].rearrange("p a b -> p (a b)"), wl[0:P, :]).then_inc(weights_loaded, 16)
            sp.dma_start(xa[:, :, :].rearrange("p a b -> p (a b)"), wl[P:D, :]).then_inc(weights_loaded, 16)
            sp.dma_start(b0_s[:, :], b0.rearrange("(a n) -> a n", a=1).to_broadcast([P, D])).then_inc(weights_loaded, 16)
            sp.dma_start(b1_s[:, :], b1.rearrange("(a n) -> a n", a=1).to_broadcast([P, D])).then_inc(weights_loaded, 16)
            sp.wait_ge(bases_made, 1)
            sp.dma_start(base_dram.rearrange("(b j) -> b j", b=BLOCKS), gmin_i[:, :]).then_inc(bases_stored, 16)
            sp.wait_ge(bases_stored, 16)
            sp.dma_start(base_row[:, :], base_dram.rearrange("(a n) -> a n", a=1)).then_inc(bases_loaded, 16)
            for c in range(NW // XCH):
                sp.wait_ge(x_scaled, c + 1)
                sp.dma_start(table[0][c * XCH * P:(c + 1) * XCH * P, :].rearrange("(w p) f -> p w f", p=P),
                             x_all[:, c * XCH:(c + 1) * XCH, :]).then_inc(table_stored[c], 16)
            sp.sem_inc(stored[0], 16)
            sp.sem_inc(stored[1], 16)

            def load_x(layer, m, w, s):
                sp.wait_ge(node_done[s], node_no(layer, m) + 1)
                if layer == 1:
                    rows = table[1][bass.ds(w * P, P), :]
                    sp.dma_start(x_t[s][:, :], rows).then_inc(x_in[s], 16)
                elif isinstance(w, int) and w == NW - 1:
                    sp.dma_start(x_t[s][0:LAST_ROWS, :], x[w * P:NODES, :]).then_inc(x_in[s], 16)
                else:
                    sp.dma_start(x_t[s][:, :], x[bass.ds(w * P, P), :]).then_inc(x_in[s], 16)

            def store(layer, m, w, s):
                sp.wait_ge(out_ready[s], node_no(layer, m) + 1)
                if layer == 0:
                    sp.dma_start(table[1][bass.ds(w * P, P), :], out_t[s][:, :]).then_inc(stored[s], 16)
                elif isinstance(w, int) and w == NW - 1:
                    sp.dma_start(out[w * P:NODES, :], out_t[s][0:LAST_ROWS, :]).then_inc(stored[s], 16)
                else:
                    sp.dma_start(out[bass.ds(w * P, P), :], out_t[s][:, :]).then_inc(stored[s], 16)

            def pair(layer, m):
                for s in range(2):
                    load_x(layer, m, 2 * m + s, s)
                for s in range(2):
                    store(layer, m, 2 * m + s, s)

            def layer_end(layer):
                for s in range(2):
                    sp.wait_ge(stored[s], 16 * ((layer + 1) * ROUNDS + 1))
                if layer == 0:
                    sp.sem_inc(table1_whole, 1)

            def slow_pair(layer, m):
                for s in range(2):
                    load_x(layer, m, 2 * m + s, s)
                    sp.wait_ge(node_done[1 - s], node_no(layer, m) + 1 + s)
                    sp.dma_start(sums_t[:, :], sums_dram[layer][bass.ds((2 * m + s) * P, P), :]).then_inc(sums_in, 16)
                    store(layer, m, 2 * m + s, s)

            sp.wait_ge(flag_made, 1)
            disordered = sp.value_load(flag[0:1, 0:1], min_val=0, max_val=1)
            with sp.If(disordered == 0):
                for layer in range(2):
                    with sp.Fori(0, ROUNDS - 1) as m:
                        pair(layer, m)
                    pair(layer, ROUNDS - 1)
                    layer_end(layer)
            with sp.Else():
                sp.wait_ge(acc_zeroed, 1)
                for n in range(2):
                    sp.dma_start(sums_dram[n][0:NPAD, :].rearrange("(p w) f -> p (w f)", p=P),
                                 big[:, 0:NW * D]).then_inc(sums_zeroed, 16)
                    sp.dma_start(sums_dram[n][NPAD:NPAD + P, :], zeros[:, :]).then_inc(sums_zeroed, 16)
                for layer in range(2):
                    sp.wait_ge(row_added, 16 * ((layer + 1) * TILES + 1))
                    with sp.Fori(0, ROUNDS - 1) as m:
                        slow_pair(layer, m)
                    slow_pair(layer, ROUNDS - 1)
                    layer_end(layer)

        @block.gpsimd
        def _(g):
            nc.gpsimd.iota(count_to[:, :, :], pattern=[[1, P], [0, HB]], base=0, channel_multiplier=0,
                           allow_small_or_imprecise_dtypes=True).then_inc(consts_made, 1)
            nc.gpsimd.iota(win_iota[:, :], pattern=[[1, WIN]], base=0, channel_multiplier=0,
                           allow_small_or_imprecise_dtypes=True).then_inc(consts_made, 1)
            nc.gpsimd.iota(floor_i[:, :], pattern=[[2 * P, U // GR], [2 * P, 2], [0, GR // 2]], base=-2 * P,
                           channel_multiplier=2 * P * (U // GR)).then_inc(consts_made, 1)
            nc.gpsimd.iota(dump_row[:, :], pattern=[[0, 1]], base=DUMP, channel_multiplier=1,
                           allow_small_or_imprecise_dtypes=True).then_inc(consts_made, 1)
            nc.gpsimd.memset(ident[:, :], 0.0).then_inc(consts_made, 1)
            nc.gpsimd.memset(lower[:, :], 1.0).then_inc(consts_made, 1)
            nc.gpsimd.memset(ones[:, :], 1.0).then_inc(consts_made, 1)
            nc.gpsimd.memset(zeros[:, :], 0.0).then_inc(consts_made, 1)
            nc.gpsimd.memset(epsilon[:, :], 1e-5).then_inc(consts_made, 1)
            g.wait_ge(consts_made, 9)
            nc.gpsimd.affine_select(out=ident[:, :], in_=ident[:, :], compare_op=ALU.not_equal, fill=1.0, base=0,
                                    pattern=[[-1, P]], channel_multiplier=1).then_inc(consts_made, 1)
            nc.gpsimd.affine_select(out=lower[:, :], in_=lower[:, :], compare_op=ALU.is_gt, fill=0.0, base=0,
                                    pattern=[[-1, P]], channel_multiplier=1).then_inc(consts_made, 1)

            def gather_quarter(layer, i, q):
                g.wait_ge(idx_ready, (layer * ROUNDS + i) * 4 + q + 1)
                g.sem_inc(gather_turn, 1)
                for u in range(q * QT, (q + 1) * QT):
                    g.indirect_dma_start(ring[:, u, :], None, table[layer],
                                         bass.IndirectOffsetOnAxis(ap=idx[:, u:u + 1], axis=0)).then_inc(rows_in[u], 16)

            for c in range(NW // XCH):
                g.wait_ge(table_stored[c], 16)
            g.wait_ge(flag_made, 1)
            disordered = g.value_load(flag[0:1, 0:1], min_val=0, max_val=1)
            with g.If(disordered == 0):
                for layer in range(2):
                    if layer == 1:
                        g.wait_ge(table1_whole, 1)
                    with g.Fori(0, ROUNDS) as i:
                        for q in range(4):
                            gather_quarter(layer, i, q)
            with g.Else():
                g.wait_ge(sums_zeroed, 64)
                for layer in range(2):
                    if layer == 1:
                        g.wait_ge(table1_whole, 1)
                    with g.Fori(0, TILES) as t:
                        g.wait_ge(one_idx_ready, layer * TILES + t + 1)
                        g.sem_inc(gather_turn, 1)
                        g.indirect_dma_start(ring[:, 0, :], None, table[layer],
                                             bass.IndirectOffsetOnAxis(ap=idx[:, 0:1], axis=0)).then_inc(row_in, 16)
                        g.wait_ge(comb_ready, layer * TILES + t + 1)
                        g.sem_inc(gather_turn, 1)
                        g.indirect_dma_start(sums_dram[layer],
                                             bass.IndirectOffsetOnAxis(ap=idx[:, 1:2], axis=0), ring[:, 1, :], None,
                                             compute_op=ALU.add).then_inc(row_added, 16)

        @block.scalar
        def _(act):
            for n in range(2):
                act.wait_ge(edges_turned, 1 + n)
                cols = banks[:, 4 * n:4 * n + 4, :].rearrange("p a b -> p (a b)")[:, 0:TILES]
                nc.scalar.copy((src_col[:, 0:TILES], dst_col[:, :])[n], cols).then_inc(edges_in_cols, 1)
            act.wait_ge(consts_made, 11)
            act.drain()
            nc.scalar.copy(src_col[:, TILES:TILES + U], src_col[:, 0:U])
            nc.scalar.copy(idx[:, :], src_col[:, 0:U]).then_inc(idx_ready, 4)
            act.wait_ge(w_turned, 1)
            nc.scalar.copy(wt_s[:, :, :], banks[:, 0, :].rearrange("p (k o) -> p k o", k=KF)).then_inc(w_copied, 1)
            act.wait_ge(degree_ready, 1)
            nc.scalar.activation(r[:, :], r[:, :], ACT.Sqrt).then_inc(degree_rooted, 1)
            act.wait_ge(x_loaded, 32)
            act.wait_ge(r_made, 1)
            for c in range(NW // XCH):
                for w in range(c * XCH + 9, (c + 1) * XCH):
                    last = nc.scalar.activation(x_all[:, w, :], x_all[:, w, :], ACT.Copy, scale=r[:, w:w + 1])
                last.then_inc(x_scaled_act, 1)

            def refill(layer, i, q):
                act.wait_ge(tiles_done, (layer * ROUNDS + i) * U + q * QT + QT + U)
                act.sem_inc(act_turn, 1)
                nc.scalar.copy(idx[:, q * QT:(q + 1) * QT],
                               src_col[:, bass.ds(i * U + U + q * QT, QT)]).then_inc(idx_ready, 1)

            def node_tile(layer, m, w, s, added):
                n = node_no(layer, m)
                if added is not None:
                    act.wait_ge(groups_added, added + 2)
                    act.wait_ge(node_done[s], n + 1)
                    act.sem_inc(act_turn, 1)
                    here = acc[:, :, bass.ds(w * P, P)]
                    nc.scalar.copy(a_t[s][:, :, :], here).then_inc(a_ready[s], 1)
                    if layer == 0:
                        act.drain()
                        nc.scalar.copy(here, zeros[:, :].rearrange("p (k n) -> p k n", k=KF)).then_inc(acc_zeroed, 1)
                else:
                    act.wait_ge(sums_turned, layer * NW + 2 * m + s + 1)
                    act.wait_ge(node_done[s], n + 1)
                    act.sem_inc(act_turn, 1)
                    nc.scalar.copy(a_t[s][:, :, :],
                                   banks[:, 5, 0:D].rearrange("p (k n) -> p k n", k=KF)).then_inc(a_ready[s], 1)
                if layer == 0:
                    act.wait_ge(x_turned, 2 * m + s + 1)
                    nc.scalar.copy(xT[:, :, :],
                                   banks[:, 6, 0:D].rearrange("p (k n) -> p k n", k=KF)).then_inc(xT_ready, 1)
                    act.wait_ge(xw_done, 2 * m + s + 1)
                    nc.scalar.copy(xw[:, :], banks[:, 6, D:2 * D]).then_inc(xw_ready, 1)
                    act.wait_ge(square_ready, 2 * m + s + 1)
                    nc.scalar.activation(scal[:, 2:3], scal[:, 1:2], ACT.Sqrt).then_inc(norm_ready, 1)
                act.wait_ge(var_ready, layer * NW + 2 * m + s + 1)
                nc.scalar.activation(scal[:, 4:5], mv[:, 1:2], ACT.Sqrt, bias=epsilon[:, 0:1]).then_inc(var_rooted, 1)

            act.wait_ge(flag_made, 1)
            disordered = act.value_load(flag[0:1, 0:1], min_val=0, max_val=1)
            with act.If(disordered == 0):
                for layer in range(2):
                    for q in range(4):
                        refill(layer, 0, q)
                    with act.Fori(1, ROUNDS) as i:
                        refill(layer, i, 0)
                        refill(layer, i, 1)
                        node_tile(layer, i - 1, 2 * i - 2, 0, group_no(layer, i, GR // 2))
                        refill(layer, i, 2)
                        node_tile(layer, i - 1, 2 * i - 1, 1, group_no(layer, i, GR // 2 + 2))
                        refill(layer, i, 3)
                    for s in range(2):
                        node_tile(layer, ROUNDS - 1, NW - 2 + s, s, (layer + 1) * GROUPS)
            with act.Else():
                for layer in range(2):
                    with act.Fori(0, TILES) as t:
                        act.wait_ge(row_added, 16 * (layer * TILES + t + 1))
                        act.sem_inc(act_turn, 1)
                        nc.scalar.copy(idx[:, 0:1], src_col[:, bass.ds(t, 1)]).then_inc(one_idx_ready, 1)
                    with act.Fori(0, ROUNDS) as m:
                        for s in range(2):
                            node_tile(layer, m, None, s, None)

        @block.vector
        def _(v):
            def ordered():
                v.drain()

            def hot_batch(n, batch, half, which):
                v.wait_ge(hot_used, n + 1)
                for digit, hot, size in ((lo, lo_hot, P), (hi, hi_hot, HI)):
                    vals = digit[which][:, bass.ds(batch * HB, HB)].unsqueeze(1).to_broadcast([P, size, HB])
                    last = nc.vector.tensor_tensor(hot[half][:, :, :], vals, count_to[:, 0:size, :], ALU.is_equal)
                last.then_inc(hot_made, 1)

            v.sem_inc(node_done[0], 1)
            v.sem_inc(node_done[1], 1)
            v.sem_inc(groups_added, 2)
            last_block = (BLOCKS - 1) * P
            nc.vector.memset(nat_i[0][:, last_block:last_block + P], PAD_SRC)
            nc.vector.memset(nat_i[1][:, last_block:last_block + P], PAD_DST).then_inc(edges_padded, 1)
            nc.vector.memset(x_all[:, NW - 1, :], 0.0).then_inc(x_padded, 1)
            nc.vector.memset(deg[:, :], 0.0)
            v.wait_ge(edges_loaded, 96)
            for n in range(2):
                nc.vector.tensor_copy(nat[n], nat_i[n]).then_inc(edges_float, 1)
            ordered()
            by_tile = nat[1].rearrange("p (b e) -> p b e", b=BLOCKS)
            nc.vector.tensor_reduce(bounds[:, 0, :], by_tile, AX.X, ALU.min)
            nc.vector.tensor_reduce(bounds[:, 1, :], by_tile, AX.X, ALU.max).then_inc(bounds_made, 1)

            def digits(n, cols_i):
                nc.vector.tensor_scalar(digit_t[:, :], cols_i, P - 1, None, ALU.bitwise_and)
                ordered()
                nc.vector.tensor_copy(lo[n], digit_t[:, :])
                ordered()
                nc.vector.tensor_scalar(digit_t[:, :], cols_i, P.bit_length() - 1, None, ALU.arith_shift_right)
                ordered()
                nc.vector.tensor_copy(hi[n], digit_t[:, :])
                ordered()

            v.wait_ge(edges_in_cols, 1)
            digits(0, src_col[:, 0:TILES])
            v.wait_ge(consts_made, 11)
            hot_batch(0, 0, 0, 0)
            hot_batch(1, 1, 1, 0)
            with v.Fori(1, HBATCHES // 2) as b:
                for half in range(2):
                    hot_batch(2 * b + half, 2 * b + half, half, 0)
            v.wait_ge(bounds_turned, 1)
            for n, to in enumerate((gmin, gmax)):
                from_tiles = banks[0:BLOCKS, n, 0:P].rearrange("b (j t) -> b j t", t=GT)
                nc.vector.tensor_reduce(to[:, :], from_tiles, AX.X, (ALU.min, ALU.max)[n])
            nc.vector.tensor_copy(floor_f[:, :], floor_i[:, :])
            ordered()
            nc.vector.tensor_copy(gmin_i[:, :], gmin[:, :]).then_inc(bases_made, 1)
            nc.vector.tensor_tensor(gmax[:, :], gmax[:, :], gmin[:, :], ALU.subtract)
            nc.vector.tensor_scalar(floor_f[:, :], floor_f[:, :], float(PAD_DST), None, ALU.min)
            ordered()
            nc.vector.tensor_scalar(gmax[:, :], gmax[:, :], float(WIN - 1), None, ALU.is_gt)
            nc.vector.tensor_tensor(floor_f[:, :], gmin[:, :], floor_f[:, :], ALU.is_lt)
            ordered()
            nc.vector.tensor_tensor(gmax[:, :], gmax[:, :], floor_f[:, :], ALU.max)
            ordered()
            nc.vector.tensor_reduce(bad[:, 0:1], gmax[:, :], AX.X, ALU.max).then_inc(bad_counted, 1)
            v.wait_ge(bad_summed, 1)
            nc.vector.tensor_scalar(flag[:, :], banks[0:1, 2, 0:1], 0.0, None, ALU.is_gt).then_inc(flag_made, 1)
            v.wait_ge(hot_used, HBATCHES + 2)
            nc.vector.tensor_scalar(r[:, :], hist(0), 1.0, None, ALU.max).then_inc(degree_ready, 1)
            v.wait_ge(degree_rooted, 1)
            nc.vector.reciprocal(r[:, :], r[:, :]).then_inc(r_made, 1)
            ordered()
            v.wait_ge(x_loaded, 32)
            for c in range(NW // XCH):
                for w in range(c * XCH, c * XCH + 9):
                    nc.vector.tensor_scalar(x_all[:, w, :], x_all[:, w, :], r[:, w:w + 1], None, ALU.mult)
                ordered()
                v.wait_ge(x_scaled_act, c + 1)
                v.sem_inc(x_scaled, 1)
            v.wait_ge(bases_loaded, 16)
            nc.vector.tensor_copy(base_row_f[:, :], base_row[:, :]).then_inc(bases_float, 1)
            v.wait_ge(edges_in_cols, 2)
            nc.vector.tensor_copy(digit_t[:, :], dst_col[:, :])
            ordered()
            nc.vector.tensor_scalar(dst_rel[:, 0:TILES].bitcast(I32), digit_t[:, :], P.bit_length() - 1, None, ALU.arith_shift_right)
            ordered()
            nc.vector.tensor_copy(hi[1], dst_rel[:, 0:TILES].bitcast(I32))
            ordered()
            nc.vector.tensor_scalar(dst_rel[:, 0:TILES].bitcast(I32), digit_t[:, :], P - 1, None, ALU.bitwise_and)
            ordered()
            nc.vector.tensor_copy(lo[1], dst_rel[:, 0:TILES].bitcast(I32))
            ordered()
            v.wait_ge(bases_spread, 1)
            nc.vector.tensor_tensor(dst_rel[:, 0:TILES].rearrange("p (g t) -> p g t", t=GT),
                                    dst_col[:, :].rearrange("p (g t) -> p g t", t=GT),
                                    banks[:, 3, 0:GROUPS].unsqueeze(2).to_broadcast([P, GROUPS, GT]), ALU.subtract)
            ordered()
            nc.vector.tensor_copy(dst_rel[:, TILES:TILES + GT], dst_rel[:, 0:GT])
            ordered()

            def group_hot(first_tile, buf, after=0):
                rel = dst_rel[:, bass.ds(first_tile, GT)].unsqueeze(2).to_broadcast([P, GT, WIN])
                nc.vector.tensor_tensor(dst_hot[:, buf, :, :], win_iota[:, :].unsqueeze(1).to_broadcast([P, GT, WIN]),
                                        rel, ALU.is_equal).then_inc(dst_hot_made, 1)

            for c in range(NW // XCH):
                v.wait_ge(table_stored[c], 16)
                end = (c + 1) * XCH * D if c < NW // XCH - 1 else KF * ACC_N
                last = nc.vector.memset(big[:, c * XCH * D:end], 0.0)
            last.then_inc(acc_zeroed, 1)
            ordered()

            def add_group(layer, i, k):
                base = v.value_load(base_row[0:1, bass.ds(i * GR + k, 1)], min_val=0, max_val=NPAD)
                v.wait_ge(tiles_done, group_no(layer, i, k) * GT + GT + U)
                here = acc[:, :, bass.ds(base, WIN)]
                nc.vector.tensor_tensor(here, group_sum(k % 2), here, ALU.add).then_inc(groups_added, 1)

            def norm_out(layer, m, s):
                n = node_no(layer, m)
                nc.vector.bn_stats(stats[:, :], h[:, :])
                ordered()
                nc.vector.bn_aggr(mv[:, :], stats[:, :])
                ordered()
                v.sem_inc(var_ready, 1)
                v.wait_ge(var_rooted, layer * NW + 2 * m + s + 1)
                nc.vector.reciprocal(scal[:, 4:5], scal[:, 4:5])
                ordered()
                v.wait_ge(stored[s], 16 * (n + 1))
                nc.vector.tensor_scalar(out_t[s][:, :], h[:, :], mv[:, 0:1], scal[:, 4:5],
                                        ALU.subtract, ALU.mult).then_inc(out_ready[s], 1)
                v.sem_inc(node_done[s], 1)

            def node_tile(layer, m, w, s):
                n = node_no(layer, m)
                count = deg[:, bass.ds(w, 1)]
                if layer == 0:
                    v.wait_ge(a_ready[s], n + 1)
                    v.wait_ge(xT_ready, 2 * m + s + 1)
                    nc.vector.tensor_tensor(xa[:, :, :], xT[:, :, :], a_t[s][:, :, :], ALU.mult).then_inc(xa_ready, 1)
                    nc.vector.tensor_scalar(scal[:, 0:1], count, 1.0, None, ALU.min)
                    v.wait_ge(xw_ready, 2 * m + s + 1)
                    v.wait_ge(projected, layer * NW + 2 * m + s + 1)
                    nc.vector.scalar_tensor_tensor(e[:, :], banks[:, 7, 0:D], r[:, bass.ds(w, 1)], xw[:, :],
                                                   ALU.mult, ALU.add)
                    ordered()
                    nc.vector.scalar_tensor_tensor(e[:, :], e[:, :], scal[:, 0:1], b0_s[:, :], ALU.mult, ALU.add)
                    ordered()
                    nc.vector.scalar_tensor_tensor(e[:, :], e[:, :], 0.01, e[:, :], ALU.mult, ALU.max)
                    ordered()
                    nc.vector.tensor_tensor_reduce(out=h[:, :], in0=e[:, :], in1=e[:, :], scale=1.0, scalar=0.0,
                                                   op0=ALU.mult, op1=ALU.add, accum_out=scal[:, 1:2])
                    ordered()
                    v.sem_inc(square_ready, 1)
                    v.wait_ge(norm_ready, 2 * m + s + 1)
                    nc.vector.tensor_scalar(scal[:, 2:3], scal[:, 2:3], 1e-12, None, ALU.max)
                    ordered()
                    nc.vector.reciprocal(scal[:, 3:4], scal[:, 2:3])
                    ordered()
                    nc.vector.scalar_tensor_tensor(h[:, :], e[:, :], scal[:, 3:4], x_t[s][:, :], ALU.mult, ALU.add)
                    ordered()
                else:
                    nc.vector.tensor_scalar(scal[:, 0:1], count, 1.0, None, ALU.add)
                    ordered()
                    nc.vector.reciprocal(scal[:, 1:2], scal[:, 0:1])
                    ordered()
                    nc.vector.tensor_tensor(scal[:, 2:3], scal[:, 1:2], count, ALU.mult)
                    ordered()
                    v.wait_ge(x_in[s], 16 * (n + 1))
                    nc.vector.scalar_tensor_tensor(e[:, :], b1_s[:, :], scal[:, 2:3], x_t[s][:, :], ALU.mult, ALU.add)
                    ordered()
                    v.wait_ge(projected, layer * NW + 2 * m + s + 1)
                    nc.vector.scalar_tensor_tensor(h[:, :], banks[:, 6 + s, 0:D], scal[:, 1:2], e[:, :],
                                                   ALU.mult, ALU.add)
                    ordered()
                norm_out(layer, m, s)

            def add_hist(n, half):
                v.wait_ge(hot_used, n + 3)
                nc.vector.tensor_tensor(deg[:, :], hist(half), deg[:, :], ALU.add)
                ordered()

            def round_(layer, i, finish):
                for k in range(GR):
                    if layer == 0 and k in (0, GR // 2):
                        half = k // (GR // 2)
                        hot_batch(HBATCHES + 2 * i + half, 2 * i + half, half, 1)
                    group_hot(i * U + (k + 1) * GT, (k + 1) % 2)
                    add_group(layer, i, k)
                    ordered()
                    if layer == 0 and k in (GR // 2 - 1, GR - 1):
                        half = k // (GR // 2)
                        add_hist(HBATCHES + 2 * i + half, half)
                    if finish and k in (GR // 2 - 1, GR // 2 + 1):
                        s = (k - (GR // 2 - 1)) // 2
                        node_tile(layer, i - 1, 2 * i - 2 + s, s)

            v.wait_ge(w_copied, 1)
            v.wait_ge(weights_loaded, 96)
            v.wait_ge(flag_made, 1)
            disordered = v.value_load(flag[0:1, 0:1], min_val=0, max_val=1)
            with v.If(disordered == 0):
                group_hot(0, 0)
                for layer in range(2):
                    if layer == 1:
                        v.wait_ge(acc_zeroed, NW + 1)
                    round_(layer, 0, False)
                    with v.Fori(1, ROUNDS) as i:
                        round_(layer, i, True)
                    for s in range(2):
                        node_tile(layer, ROUNDS - 1, NW - 2 + s, s)
            with v.Else():
                v.sem_inc(row_added, 16)
                with v.Fori(0, HBATCHES // 2) as b:
                    for half in range(2):
                        hot_batch(HBATCHES + 2 * b + half, 2 * b + half, half, 1)
                    for half in range(2):
                        add_hist(HBATCHES + 2 * b + half, half)
                for layer in range(2):
                    with v.Fori(0, TILES) as t:
                        n = layer * TILES + t
                        v.wait_ge(row_added, 16 * (n + 1))
                        nc.vector.tensor_copy(scal[:, 5:6], dst_col[:, bass.ds(t, 1)]).then_inc(dcol_ready, 1)
                        ordered()
                        v.wait_ge(drow_spread, n + 1)
                        nc.vector.tensor_scalar(same(ring), banks[:, 0, 0:P], scal[:, 5:6], None,
                                                ALU.is_equal).then_inc(same_ready, 1)
                        ordered()
                        nc.vector.tensor_tensor_reduce(out=ring[:, 3, 0:P], in0=same(ring), in1=lower[:, :], scale=1.0,
                                                       scalar=0.0, op0=ALU.mult, op1=ALU.add, accum_out=scal[:, 6:7])
                        ordered()
                        nc.vector.tensor_scalar(scal[:, 6:7], scal[:, 6:7], 0.0, None, ALU.is_equal)
                        nc.vector.tensor_tensor(scal[:, 7:8], scal[:, 5:6], dump_row[:, :], ALU.subtract)
                        ordered()
                        nc.vector.scalar_tensor_tensor(scal[:, 7:8], scal[:, 7:8], scal[:, 6:7], dump_row[:, :],
                                                       ALU.mult, ALU.add)
                        ordered()
                        nc.vector.tensor_copy(idx[:, 1:2], scal[:, 7:8])
                        v.wait_ge(combined, n + 1)
                        nc.vector.tensor_copy(ring[:, 1, :], banks[:, 1, 0:D])
                        ordered()
                        v.sem_inc(comb_ready, 1)
                    with v.Fori(0, ROUNDS) as m:
                        for s in range(2):
                            node_tile(layer, m, 2 * m + s, s)

        @block.tensor
        def _(pe):
            pe.sem_inc(hot_used, 2)
            pe.sem_inc(tiles_done, U)
            pe.wait_ge(consts_made, 11)

            def turn_edges(n):
                pe.wait_ge(edges_float, n + 1)
                for b in range(BLOCKS):
                    rows = P if b < BLOCKS - 1 else LAST_BLOCK_TILES
                    last = nc.tensor.transpose(banks[:, 4 * n + b // 4, (b % 4) * P:(b % 4) * P + rows],
                                               nat[n][0:rows, b * P:(b + 1) * P], ident[0:rows, 0:rows])
                last.then_inc(edges_turned, 1)

            def hist_batch(n, half, first, last_one, bank):
                pe.wait_ge(hot_made, n + 1)
                for t in range(HB):
                    last = nc.tensor.matmul(hist(bank), lo_hot[half][:, :, t], hi_hot[half][:, :, t],
                                            start=first and t == 0, stop=last_one and t == HB - 1)
                last.then_inc(hot_used, 1)

            turn_edges(0)
            turn_edges(1)
            pe.wait_ge(bounds_made, 1)
            pe.wait_ge(edges_in_cols, 1)
            for n in range(2):
                last = nc.tensor.transpose(banks[0:BLOCKS, n, 0:P], bounds[:, n, :], ident[:, :])
            last.then_inc(bounds_turned, 1)
            pe.wait_ge(edges_in_cols, 2)
            hist_batch(0, 0, True, False, 0)
            hist_batch(1, 1, False, False, 0)
            with pe.Fori(1, HBATCHES // 2 - 1) as b:
                for half in range(2):
                    hist_batch(2 * b + half, half, False, False, 0)
            hist_batch(HBATCHES - 2, 0, False, False, 0)
            hist_batch(HBATCHES - 1, 1, False, True, 0)
            pe.wait_ge(bad_counted, 1)
            nc.tensor.matmul(banks[0:1, 2, 0:1], bad[:, 0:1], ones[0:BLOCKS, 0:1],
                             start=True, stop=True).then_inc(bad_summed, 1)
            pe.wait_ge(weights_loaded, 96)
            for o, half in enumerate((xT, xa)):
                for k in range(KF):
                    last = nc.tensor.transpose(banks[:, 0, k * D + o * P:k * D + (o + 1) * P], half[:, k, :], ident[:, :])
            last.then_inc(w_turned, 1)
            pe.wait_ge(bases_float, 1)
            nc.tensor.matmul(banks[:, 3, 0:GROUPS], ones[0:1, :], base_row_f[:, 0:GROUPS],
                             start=True, stop=True).then_inc(bases_spread, 1)

            def node_tile(layer, m, w, s):
                n = node_no(layer, m)
                if layer == 0:
                    pe.wait_ge(x_in[s], 16 * (n + 1))
                    for k in range(KF):
                        last = nc.tensor.transpose(banks[:, 6, k * P:(k + 1) * P], x_t[s][:, k * P:(k + 1) * P],
                                                   ident[:, :])
                    last.then_inc(x_turned, 1)
                    pe.wait_ge(xT_ready, 2 * m + s + 1)
                    pe.wait_ge(xa_ready, 2 * m + s + 1)
                    for k in range(KF):
                        last = nc.tensor.matmul(banks[:, 6, D:2 * D], xT[:, k, :], w1_s[:, k, :],
                                                start=k == 0, stop=k == KF - 1)
                    last.then_inc(xw_done, 1)
                    parts = [(a_t[s][:, k, :], w1_s[:, k, :]) for k in range(KF)]
                    parts += [(xa[:, k, :], w2_s[:, k, :]) for k in range(KF)]
                    to = banks[:, 7, 0:D]
                    pe.wait_ge(xw_ready, 2 * m + s + 1)
                else:
                    pe.wait_ge(a_ready[s], n + 1)
                    parts = [(a_t[s][:, k, :], wt_s[:, k, :]) for k in range(KF)]
                    to = banks[:, 6 + s, 0:D]
                for k, (left, right) in enumerate(parts):
                    last = nc.tensor.matmul(to, left, right, start=k == 0, stop=k == len(parts) - 1)
                last.then_inc(projected, 1)

            def round_(layer, i, finish):
                for k in range(GR):
                    if layer == 0 and k in (0, GR // 2):
                        half = k // (GR // 2)
                        hist_batch(HBATCHES + 2 * i + half, half, True, True, half)
                    pe.wait_ge(dst_hot_made, group_no(layer, i, k) + 1)
                    pe.wait_ge(groups_added, group_no(layer, i, k) + 1)
                    for j in range(GT):
                        u = k * GT + j
                        pe.wait_ge(rows_in[u], 16 * (layer * ROUNDS + i + 1))
                        for f in range(KF):
                            last = nc.tensor.matmul(group_sum(k % 2)[:, f, :], ring[:, u, f * P:(f + 1) * P],
                                                    dst_hot[:, k % 2, j, :], start=j == 0, stop=j == GT - 1)
                        last.then_inc(tiles_done, 1)
                    if finish and k in (GR // 2 - 1, GR // 2 + 1):
                        s = (k - (GR // 2 - 1)) // 2
                        node_tile(layer, i - 1, 2 * i - 2 + s, s)

            pe.wait_ge(r_made, 1)
            pe.wait_ge(w_copied, 1)
            pe.wait_ge(flag_made, 1)
            disordered = pe.value_load(flag[0:1, 0:1], min_val=0, max_val=1)
            with pe.If(disordered == 0):
                for layer in range(2):
                    round_(layer, 0, False)
                    with pe.Fori(1, ROUNDS) as i:
                        round_(layer, i, True)
                    for s in range(2):
                        node_tile(layer, ROUNDS - 1, NW - 2 + s, s)
            with pe.Else():
                with pe.Fori(0, HBATCHES // 2) as b:
                    for half in range(2):
                        hist_batch(HBATCHES + 2 * b + half, half, True, True, half)
                for layer in range(2):
                    with pe.Fori(0, TILES) as t:
                        n = layer * TILES + t
                        pe.wait_ge(dcol_ready, n + 1)
                        nc.tensor.matmul(banks[:, 0, 0:P], scal[:, 5:6].to_broadcast([P, P]), ident[:, :],
                                         start=True, stop=True).then_inc(drow_spread, 1)
                        pe.wait_ge(same_ready, n + 1)
                        pe.wait_ge(row_in, 16 * (n + 1))
                        nc.tensor.matmul(banks[:, 1, 0:D], same(ring), ring[:, 0, :],
                                         start=True, stop=True).then_inc(combined, 1)
                    with pe.Fori(0, ROUNDS) as m:
                        for s in range(2):
                            pe.wait_ge(sums_in, 16 * (layer * NW + 2 * m + s + 1))
                            for k in range(KF):
                                last = nc.tensor.transpose(banks[:, 5, k * P:(k + 1) * P],
                                                           sums_t[:, k * P:(k + 1) * P], ident[:, :])
                            last.then_inc(sums_turned, 1)
                            node_tile(layer, m, None, s)


def same(ring):
    return ring[:, 2, 0:P]


_INS = ["x", "src", "dst", "L0_gnn_W1", "L0_gnn_W2", "L0_gnn_b", "L1_gnn_W", "L1_gnn_b"]


def kernel(**inputs):
    import numpy as np
    import concourse.bacc as bacc
    from concourse import mybir as mb
    from concourse.bass_utils import run_bass_kernel_spmd

    nc = bacc.Bacc("TRN2", target_bir_lowering=False, num_devices=1)
    arrays, args = {}, []
    for name in _INS:
        a = np.ascontiguousarray(inputs[name])
        arrays[f"in_{name}"] = a
        args.append(nc.dram_tensor(f"in_{name}", a.shape, mb.dt.from_np(a.dtype), kind="ExternalInput").ap())
    result = nc.dram_tensor("result", (NODES, D), mb.dt.float32, kind="ExternalOutput").ap()
    gnn(nc, *args, result)
    r = run_bass_kernel_spmd(nc, [arrays], core_ids=[0])
    return r.results[0]["result"]
```

```python
import concourse.bass as bass
from concourse import mybir
from contextlib import ExitStack

F32, BF16, I32 = mybir.dt.float32, mybir.dt.bfloat16, mybir.dt.int32
ALU = mybir.AluOpType
ACT = mybir.ActivationFunctionType
AX = mybir.AxisListType

P = 128
D = 256
KF = D // P
NODES = 12500
EDGES = 200000
NW = -(-NODES // P)
NPAD = NW * P
LAST_ROWS = NODES - (NW - 1) * P
ROUNDS = NW // 2
U = 32
TILES = ROUNDS * U
GT = 4
GR = U // GT
GROUPS = TILES // GT
WIN = 64
ACC_N = NPAD + WIN
BLOCKS = -(-TILES // P)
FULL_TILES = EDGES // P
LAST_EDGES = EDGES - FULL_TILES * P
LAST_BLOCK_TILES = TILES - (BLOCKS - 1) * P
PAD_SRC = NPAD - 1
PAD_DST = NODES
HB = 16
HBATCHES = TILES // HB
HI = NW
LAST_K = 3
AHEAD = 2
HOTS = 4
QT = U // 4
XCH = 14
DUMP = NPAD


def gnn(nc, x, src, dst, w1, w2, b0, wl, b1, out):
    table = [nc.dram_tensor("scaled_x", (NPAD, D), F32, kind="Internal").ap(),
             nc.dram_tensor("x1", (NPAD, D), F32, kind="Internal").ap()]
    base_dram = nc.dram_tensor("group_bases", (BLOCKS * U,), I32, kind="Internal").ap()
    sums_dram = [nc.dram_tensor(f"sums{n}", (NPAD + P, D), F32, kind="Internal").ap() for n in range(2)]

    with ExitStack() as ctx:
        def sb(name, shape, dt=F32):
            return ctx.enter_context(nc.sbuf_tensor(name, shape, dt))

        def sem(name):
            return ctx.enter_context(nc.semaphore(name))

        big = sb("big", [P, KF * ACC_N])
        acc = big[:, :].rearrange("p (k n) -> p k n", k=KF)
        x_all = big[:, 0:NW * D].rearrange("p (w f) -> p w f", w=NW)
        ring = sb("ring", [P, U, D])
        ring_flat = ring[:, :, :].rearrange("p u f -> p (u f)")
        nat = [ring_flat[:, n * BLOCKS * P:(n + 1) * BLOCKS * P] for n in range(2)]
        nat_i = [ring_flat[:, (2 + n) * BLOCKS * P:(3 + n) * BLOCKS * P].bitcast(I32) for n in range(2)]
        src_col = sb("src_col", [P, TILES + U], I32)
        dst_col = sb("dst_col", [P, TILES])
        dst_rel = sb("dst_rel", [P, TILES + AHEAD * GT])
        src_digits = ring_flat[:, 2 * BLOCKS * P:3 * BLOCKS * P].bitcast(BF16)
        lo = [src_digits[:, 0:TILES], sb("dst_lo", [P, TILES + HB], BF16)[:, :]]
        hi = [src_digits[:, TILES:2 * TILES], sb("dst_hi", [P, TILES + HB], BF16)[:, :]]
        count_to = sb("count_to", [P, P, HB], BF16)
        hot = sb("hot", [P, 2, P + HI, HB], BF16)
        lo_hot = [hot[:, n, 0:P, :] for n in range(2)]
        hi_hot = [hot[:, n, P:P + HI, :] for n in range(2)]
        digit_t = hot[:, :, :, :].rearrange("p a b c -> p (a b c)")[:, 0:2 * TILES].bitcast(I32)
        win_iota = sb("win_iota", [P, WIN])
        dst_hot = sb("dst_hot", [P, HOTS, GT, WIN])
        idx = sb("idx", [P, U], I32)
        ident = sb("ident", [P, P])
        lower = sb("lower", [P, P])
        ones = sb("ones", [P, P])
        zeros = sb("zeros", [P, D])
        dump_row = sb("dump_row", [P, 1])
        epsilon = sb("epsilon", [P, 1])
        bounds = sb("bounds", [P, 2, BLOCKS])
        gmin = sb("gmin", [BLOCKS, U])
        gmax = sb("gmax", [BLOCKS, U])
        floor_i = sb("floor_i", [BLOCKS, U], I32)
        floor_late = sb("floor_late", [BLOCKS, U // GR, GR - LAST_K - 1], I32)
        floor_f = sb("floor_f", [BLOCKS, U])
        gmin_i = sb("gmin_i", [BLOCKS, U], I32)
        bad = sb("bad", [BLOCKS, 4])
        flag = sb("flag", [1, 1], I32)
        base_row = sb("base_row", [1, BLOCKS * U], I32)
        base_row_f = dst_hot[0:1, 0:2, :, :].rearrange("p a b c -> p (a b c)")[:, 0:BLOCKS * U]
        r = sb("r", [P, NW])
        root = sb("root", [P, NW])
        r_diag = [sb(f"r_diag{n}", [P, P]) for n in range(2)]
        deg = sb("deg", [P, NW])
        w1_s = sb("w1_s", [P, KF, D])
        w2_s = sb("w2_s", [P, KF, D])
        wt_s = sb("wt_s", [P, KF, D])
        b0_s = sb("b0_s", [P, D])
        b1_s = sb("b1_s", [P, D])
        x_t = [sb(f"x_t{n}", [P, D]) for n in range(2)]
        a_t = [sb(f"a_t{n}", [P, KF, P]) for n in range(2)]
        out_t = [sb(f"out_t{n}", [P, D]) for n in range(2)]
        sums_t = sb("sums_t", [P, D])
        sum_a = a_t
        xa = [sb(f"xa{n}", [P, KF, P]) for n in range(2)]
        e = [sb(f"e{n}", [P, D]) for n in range(2)]
        scal = sb("scal", [P, 8])
        pair = [scal[:, 2 * n:2 * n + 2] for n in range(4)]
        stats = sb("stats", [P, 2, 6])
        mv = sb("mv", [P, 2, 2])

        banks = ctx.enter_context(nc.psum_tensor("banks", [P, 8, 512], F32))

        def group_sum(buf):
            return banks[:, 2 * buf:2 * buf + 2, 0:WIN]

        hist = banks[:, 4, 0:HI]
        turned = [banks[:, 5 + s, :].rearrange("p (a k n) -> p a k n", a=2, k=KF) for s in range(2)]
        project = [banks[:, 7, 0:D], banks[:, 5, 0:D]]

        consts_made = sem("consts_made")
        edges_loaded = sem("edges_loaded")
        edges_padded = sem("edges_padded")
        weights_loaded = sem("weights_loaded")
        x_loaded = sem("x_loaded")
        x_padded = sem("x_padded")
        edges_float = sem("edges_float")
        edges_turned = sem("edges_turned")
        edges_in_cols = sem("edges_in_cols")
        bounds_made = sem("bounds_made")
        bounds_turned = sem("bounds_turned")
        bad_counted = sem("bad_counted")
        bad_summed = sem("bad_summed")
        bases_made = sem("bases_made")
        bases_stored = sem("bases_stored")
        bases_loaded = sem("bases_loaded")
        bases_float = sem("bases_float")
        bases_spread = sem("bases_spread")
        flag_made = sem("flag_made")
        w_turned = sem("w_turned")
        w_copied = sem("w_copied")
        hot_made = sem("hot_made")
        hot_used = sem("hot_used")
        degree_ready = sem("degree_ready")
        degree_rooted = sem("degree_rooted")
        r_made = sem("r_made")
        x_scaled_act = sem("x_scaled_act")
        x_scaled = sem("x_scaled")
        table_stored = [sem(f"table_stored{c}") for c in range(NW // XCH)]
        acc_zeroed = sem("acc_zeroed")
        idx_ready = sem("idx_ready")
        rows_in = [sem(f"rows_in{u}") for u in range(U)]
        gather_turn = sem("gather_turn")
        dst_hot_made = sem("dst_hot_made")
        tiles_done = sem("tiles_done")
        groups_added = sem("groups_added")
        act_turn = sem("act_turn")
        x_in = [sem(f"x_in{n}") for n in range(2)]
        sums_in = sem("sums_in")
        stored = [sem(f"stored{n}") for n in range(2)]
        out_ready = [sem(f"out_ready{n}") for n in range(2)]
        a_ready = [sem(f"a_ready{n}") for n in range(2)]
        diag_ready = sem("diag_ready")
        x_turned = sem("x_turned")
        sums_turned = sem("sums_turned")
        mixed = sem("mixed")
        hist_added = sem("hist_added")
        projected = sem("projected")
        square_ready = sem("square_ready")
        norm_ready = sem("norm_ready")
        var_ready = sem("var_ready")
        var_rooted = sem("var_rooted")
        table1_whole = sem("table1_whole")
        dcol_ready = sem("dcol_ready")
        drow_spread = sem("drow_spread")
        same_ready = sem("same_ready")
        to_ready = sem("to_ready")
        combined = sem("combined")
        comb_ready = sem("comb_ready")
        one_idx_ready = sem("one_idx_ready")
        row_in = sem("row_in")
        row_added = sem("row_added")
        tile_over = sem("tile_over")
        sums_zeroed = sem("sums_zeroed")

        block = ctx.enter_context(nc.Block())

        def group_no(layer, i, k):
            return layer * GROUPS + i * GR + k

        def node_no(layer, m):
            return layer * ROUNDS + m

        @block.sync
        def _(sp):
            sp.wait_ge(edges_padded, 1)
            for n, edges in enumerate((src, dst)):
                whole = (BLOCKS - 1) * P
                v = nat_i[n].rearrange("p (b e) -> p b e", b=BLOCKS)
                sp.dma_start(v[:, 0:BLOCKS - 1, :],
                             edges[0:whole * P].rearrange("(b p e) -> p b e", p=P, e=P)).then_inc(edges_loaded, 16)
                sp.dma_start(v[0:FULL_TILES - whole, BLOCKS - 1, :],
                             edges[whole * P:FULL_TILES * P].rearrange("(p e) -> p e", e=P)).then_inc(edges_loaded, 16)
                sp.dma_start(v[FULL_TILES - whole:FULL_TILES - whole + 1, BLOCKS - 1, 0:LAST_EDGES],
                             edges[FULL_TILES * P:EDGES].rearrange("(p e) -> p e", p=1)).then_inc(edges_loaded, 16)
            sp.wait_ge(x_padded, 1)
            x_rows = x[0:(NW - 1) * P, :].rearrange("(w p) f -> p w f", p=P)
            sp.dma_start(x_all[:, 0:NW - 1, :], x_rows).then_inc(x_loaded, 16)
            sp.dma_start(x_all[0:LAST_ROWS, NW - 1, :], x[(NW - 1) * P:NODES, :]).then_inc(x_loaded, 16)
            sp.dma_start(w1_s[:, :, :], w1.rearrange("(k p) n -> p k n", p=P)).then_inc(weights_loaded, 16)
            sp.dma_start(w2_s[:, :, :], w2.rearrange("(k p) n -> p k n", p=P)).then_inc(weights_loaded, 16)
            sp.dma_start(xa[0][:, :, :].rearrange("p a b -> p (a b)"), wl[0:P, :]).then_inc(weights_loaded, 16)
            sp.dma_start(xa[1][:, :, :].rearrange("p a b -> p (a b)"), wl[P:D, :]).then_inc(weights_loaded, 16)
            sp.dma_start(b0_s[:, :], b0.rearrange("(a n) -> a n", a=1).to_broadcast([P, D])).then_inc(weights_loaded, 16)
            sp.dma_start(b1_s[:, :], b1.rearrange("(a n) -> a n", a=1).to_broadcast([P, D])).then_inc(weights_loaded, 16)
            sp.wait_ge(bases_made, 1)
            sp.dma_start(base_dram.rearrange("(b j) -> b j", b=BLOCKS), gmin_i[:, :]).then_inc(bases_stored, 16)
            sp.wait_ge(bases_stored, 16)
            sp.dma_start(base_row[:, :], base_dram.rearrange("(a n) -> a n", a=1)).then_inc(bases_loaded, 16)
            for c in range(NW // XCH):
                sp.wait_ge(x_scaled, c + 1)
                sp.dma_start(table[0][c * XCH * P:(c + 1) * XCH * P, :].rearrange("(w p) f -> p w f", p=P),
                             x_all[:, c * XCH:(c + 1) * XCH, :]).then_inc(table_stored[c], 16)
            def load_x(layer, m, w, s):
                if layer == 1:
                    rows = table[1][bass.ds(w * P, P), :]
                    sp.dma_start(x_t[s][:, :], rows).then_inc(x_in[s], 16)
                elif isinstance(w, int) and w == NW - 1:
                    sp.dma_start(x_t[s][0:LAST_ROWS, :], x[w * P:NODES, :]).then_inc(x_in[s], 16)
                else:
                    sp.dma_start(x_t[s][:, :], x[bass.ds(w * P, P), :]).then_inc(x_in[s], 16)

            def store(layer, m, w, s):
                sp.wait_ge(out_ready[s], node_no(layer, m) + 1)
                if layer == 0:
                    sp.dma_start(table[1][bass.ds(w * P, P), :], out_t[s][:, :]).then_inc(stored[s], 16)
                elif isinstance(w, int) and w == NW - 1:
                    sp.dma_start(out[w * P:NODES, :], out_t[s][0:LAST_ROWS, :]).then_inc(stored[s], 16)
                else:
                    sp.dma_start(out[bass.ds(w * P, P), :], out_t[s][:, :]).then_inc(stored[s], 16)

            def next_pair(layer, m):
                for s in range(2):
                    store(layer, m, 2 * m + s, s)
                for s in range(2):
                    sp.wait_ge(stored[s], 16 * (node_no(layer, m) + 1))
                    load_x(layer, m + 1, 2 * m + 2 + s, s)

            def layer_end(layer):
                for s in range(2):
                    sp.wait_ge(stored[s], 16 * (layer + 1) * ROUNDS)
                if layer == 0:
                    sp.sem_inc(table1_whole, 1)

            def sum_rows(layer, m, s, w):
                if not (layer == 0 and s == 0 and isinstance(m, int)):
                    sp.wait_ge(sums_turned, layer * NW + 2 * m + s)
                sp.dma_start(sums_t[:, :], sums_dram[layer][bass.ds(w * P, P), :]).then_inc(sums_in, 16)

            sp.wait_ge(flag_made, 1)
            disordered = sp.value_load(flag[0:1, 0:1], min_val=0, max_val=1)
            with sp.If(disordered == 0):
                for layer in range(2):
                    for s in range(2):
                        load_x(layer, 0, s, s)
                    with sp.Fori(0, ROUNDS - 2) as m:
                        next_pair(layer, m)
                    next_pair(layer, ROUNDS - 2)
                    for s in range(2):
                        store(layer, ROUNDS - 1, NW - 2 + s, s)
                    layer_end(layer)
            with sp.Else():
                sp.wait_ge(acc_zeroed, 1)
                for n in range(2):
                    sp.dma_start(sums_dram[n][0:NPAD, :].rearrange("(p w) f -> p (w f)", p=P),
                                 big[:, 0:NW * D]).then_inc(sums_zeroed, 16)
                    sp.dma_start(sums_dram[n][NPAD:NPAD + P, :], zeros[:, :]).then_inc(sums_zeroed, 16)
                for layer in range(2):
                    sp.wait_ge(tile_over, (layer + 1) * TILES + 1)
                    for s in range(2):
                        load_x(layer, 0, s, s)
                    for s in range(2):
                        sum_rows(layer, 0, s, s)
                    with sp.Fori(0, ROUNDS - 2) as m:
                        next_pair(layer, m)
                        for s in range(2):
                            sum_rows(layer, m + 1, s, 2 * m + 2 + s)
                    next_pair(layer, ROUNDS - 2)
                    for s in range(2):
                        sum_rows(layer, ROUNDS - 1, s, NW - 2 + s)
                    for s in range(2):
                        store(layer, ROUNDS - 1, NW - 2 + s, s)
                    layer_end(layer)

        @block.gpsimd
        def _(g):
            nc.gpsimd.iota(count_to[:, :, :], pattern=[[1, P], [0, HB]], base=0, channel_multiplier=0,
                           allow_small_or_imprecise_dtypes=True).then_inc(consts_made, 1)
            nc.gpsimd.iota(win_iota[:, :], pattern=[[1, WIN]], base=0, channel_multiplier=0,
                           allow_small_or_imprecise_dtypes=True).then_inc(consts_made, 1)
            nc.gpsimd.iota(floor_i[:, :], pattern=[[2 * P, U // GR], [0, GR]], base=-2 * P,
                           channel_multiplier=2 * P * (U // GR)).then_inc(consts_made, 1)
            nc.gpsimd.iota(floor_late[:, :, :], pattern=[[2 * P, U // GR], [0, GR - LAST_K - 1]], base=0,
                           channel_multiplier=2 * P * (U // GR)).then_inc(consts_made, 1)
            nc.gpsimd.iota(dump_row[:, :], pattern=[[0, 1]], base=DUMP, channel_multiplier=1,
                           allow_small_or_imprecise_dtypes=True).then_inc(consts_made, 1)
            nc.gpsimd.memset(ident[:, :], 0.0).then_inc(consts_made, 1)
            nc.gpsimd.memset(lower[:, :], 1.0).then_inc(consts_made, 1)
            nc.gpsimd.memset(ones[:, :], 1.0).then_inc(consts_made, 1)
            nc.gpsimd.memset(zeros[:, :], 0.0).then_inc(consts_made, 1)
            nc.gpsimd.memset(epsilon[:, :], 1e-5).then_inc(consts_made, 1)
            g.wait_ge(consts_made, 10)
            nc.gpsimd.affine_select(out=ident[:, :], in_=ident[:, :], compare_op=ALU.not_equal, fill=1.0, base=0,
                                    pattern=[[-1, P]], channel_multiplier=1).then_inc(consts_made, 1)
            nc.gpsimd.affine_select(out=lower[:, :], in_=lower[:, :], compare_op=ALU.is_gt, fill=0.0, base=0,
                                    pattern=[[-1, P]], channel_multiplier=1).then_inc(consts_made, 1)

            def gather_quarter(layer, i, q):
                g.wait_ge(idx_ready, (layer * ROUNDS + i) * 4 + q + 1)
                g.sem_inc(gather_turn, 1)
                for u in range(q * QT, (q + 1) * QT):
                    g.indirect_dma_start(ring[:, u, :], None, table[layer],
                                         bass.IndirectOffsetOnAxis(ap=idx[:, u:u + 1], axis=0)).then_inc(rows_in[u], 16)

            for c in range(NW // XCH):
                g.wait_ge(table_stored[c], 16)
            g.wait_ge(flag_made, 1)
            disordered = g.value_load(flag[0:1, 0:1], min_val=0, max_val=1)
            with g.If(disordered == 0):
                for layer in range(2):
                    if layer == 1:
                        g.wait_ge(table1_whole, 1)
                    with g.Fori(0, ROUNDS) as i:
                        for q in range(4):
                            gather_quarter(layer, i, q)
            with g.Else():
                g.wait_ge(sums_zeroed, 64)
                for layer in range(2):
                    if layer == 1:
                        g.wait_ge(table1_whole, 1)
                    with g.Fori(0, TILES) as t:
                        g.wait_ge(one_idx_ready, layer * TILES + t + 1)
                        g.sem_inc(gather_turn, 1)
                        g.indirect_dma_start(ring[:, 0, :], None, table[layer],
                                             bass.IndirectOffsetOnAxis(ap=idx[:, 0:1], axis=0)).then_inc(row_in, 16)
                        g.wait_ge(comb_ready, layer * TILES + t + 1)
                        g.sem_inc(gather_turn, 1)
                        g.indirect_dma_start(sums_dram[layer],
                                             bass.IndirectOffsetOnAxis(ap=idx[:, 1:2], axis=0), ring[:, 1, :], None,
                                             compute_op=ALU.add).then_inc(row_added, 16)
                        g.wait_ge(row_added, 16 * (layer * TILES + t + 1))
                        g.sem_inc(tile_over, 1)

        @block.scalar
        def _(act):
            for n in range(2):
                act.wait_ge(edges_turned, 1 + n)
                cols = banks[:, 4 * n:4 * n + 4, :].rearrange("p a b -> p (a b)")[:, 0:TILES]
                nc.scalar.copy((src_col[:, 0:TILES], dst_col[:, :])[n], cols).then_inc(edges_in_cols, 1)
            act.wait_ge(consts_made, 12)
            act.drain()
            nc.scalar.copy(src_col[:, TILES:TILES + U], src_col[:, 0:U])
            nc.scalar.copy(idx[:, :], src_col[:, 0:U]).then_inc(idx_ready, 4)
            act.wait_ge(w_turned, 1)
            nc.scalar.copy(wt_s[:, :, :], banks[:, 0, :].rearrange("p (k o) -> p k o", k=KF)).then_inc(w_copied, 1)
            act.wait_ge(degree_ready, 1)
            nc.scalar.activation(root[:, :], r[:, :], ACT.Sqrt).then_inc(degree_rooted, 1)
            act.wait_ge(x_loaded, 32)
            act.wait_ge(r_made, 1)
            for c in range(NW // XCH):
                for w in range(c * XCH + 9, (c + 1) * XCH):
                    last = nc.scalar.activation(x_all[:, w, :], x_all[:, w, :], ACT.Copy, scale=r[:, w:w + 1])
                last.then_inc(x_scaled_act, 1)

            def refill(layer, i, q):
                act.wait_ge(tiles_done, (layer * ROUNDS + i) * U + q * QT + QT + U)
                act.sem_inc(act_turn, 1)
                nc.scalar.copy(idx[:, q * QT:(q + 1) * QT],
                               src_col[:, bass.ds(i * U + U + q * QT, QT)]).then_inc(idx_ready, 1)

            def clear_sums(m, s):
                act.wait_ge(mixed, 2 * m + s + 1)
                act.sem_inc(act_turn, 1)
                nc.scalar.copy(acc[:, :, bass.ds((2 * m + s) * P, P)],
                               zeros[:, :].rearrange("p (k n) -> p k n", k=KF)).then_inc(acc_zeroed, 1)

            def take_sums(m, s, added):
                act.wait_ge(groups_added, added + 2)
                act.sem_inc(act_turn, 1)
                nc.scalar.copy(a_t[s][:, :, :], acc[:, :, bass.ds((2 * m + s) * P, P)]).then_inc(a_ready[s], 1)

            def roots(layer, m):
                if layer == 0:
                    act.wait_ge(square_ready, m + 1)
                    nc.scalar.activation(pair[2], pair[1], ACT.Sqrt).then_inc(norm_ready, 1)
                act.wait_ge(var_ready, node_no(layer, m) + 1)
                nc.scalar.activation(pair[3], mv[:, :, 1], ACT.Sqrt, bias=epsilon[:, 0:1]).then_inc(var_rooted, 1)

            def round_(layer, i, finish):
                for q in range(4):
                    refill(layer, i, q)
                    for s in range(2 if finish and q == 1 else 0):
                        if layer == 0:
                            clear_sums(i - 1, s)
                        else:
                            take_sums(i - 1, s, group_no(layer, i, LAST_K + 1))
                    if finish and q == 2:
                        roots(layer, i - 1)

            act.wait_ge(flag_made, 1)
            disordered = act.value_load(flag[0:1, 0:1], min_val=0, max_val=1)
            with act.If(disordered == 0):
                for layer in range(2):
                    round_(layer, 0, False)
                    with act.Fori(1, ROUNDS) as i:
                        round_(layer, i, True)
                    for s in range(2):
                        if layer == 0:
                            clear_sums(ROUNDS - 1, s)
                        else:
                            take_sums(ROUNDS - 1, s, (layer + 1) * GROUPS)
                    roots(layer, ROUNDS - 1)
            with act.Else():
                for layer in range(2):
                    with act.Fori(0, TILES) as t:
                        act.wait_ge(tile_over, layer * TILES + t + 1)
                        act.sem_inc(act_turn, 1)
                        nc.scalar.copy(idx[:, 0:1], src_col[:, bass.ds(t, 1)]).then_inc(one_idx_ready, 1)
                    with act.Fori(0, ROUNDS) as m:
                        for s in range(2):
                            act.wait_ge(sums_turned, layer * NW + 2 * m + s + 1)
                            nc.scalar.copy(a_t[s][:, :, :],
                                           banks[:, 0, 0:D].rearrange("p (k n) -> p k n", k=KF)).then_inc(a_ready[s], 1)
                        roots(layer, m)

        @block.vector
        def _(v):
            def ordered():
                v.drain()

            def hot_batch(n, batch, half, which):
                v.wait_ge(hot_used, n + 1)
                for digit, hots, size in ((lo, lo_hot, P), (hi, hi_hot, HI)):
                    vals = digit[which][:, bass.ds(batch * HB, HB)].unsqueeze(1).to_broadcast([P, size, HB])
                    last = nc.vector.tensor_tensor(hots[half], vals, count_to[:, 0:size, :], ALU.is_equal)
                last.then_inc(hot_made, 1)

            v.sem_inc(groups_added, 2)
            v.sem_inc(hist_added, 1)
            last_block = (BLOCKS - 1) * P
            nc.vector.memset(nat_i[0][:, last_block:last_block + P], PAD_SRC)
            nc.vector.memset(nat_i[1][:, last_block:last_block + P], PAD_DST).then_inc(edges_padded, 1)
            nc.vector.memset(x_all[:, NW - 1, :], 0.0).then_inc(x_padded, 1)
            nc.vector.memset(deg[:, :], 0.0)
            for digit in (lo[1], hi[1]):
                nc.vector.memset(digit[:, TILES:TILES + HB], 0.0)
            v.wait_ge(edges_loaded, 96)
            for n in range(2):
                nc.vector.tensor_copy(nat[n], nat_i[n]).then_inc(edges_float, 1)
            ordered()
            by_tile = nat[1].rearrange("p (b e) -> p b e", b=BLOCKS)
            nc.vector.tensor_reduce(bounds[:, 0, :], by_tile, AX.X, ALU.min)
            nc.vector.tensor_reduce(bounds[:, 1, :], by_tile, AX.X, ALU.max).then_inc(bounds_made, 1)

            def digits(n, cols_i):
                nc.vector.tensor_scalar(digit_t[:, :], cols_i, P - 1, None, ALU.bitwise_and)
                ordered()
                nc.vector.tensor_copy(lo[n], digit_t[:, :])
                ordered()
                nc.vector.tensor_scalar(digit_t[:, :], cols_i, P.bit_length() - 1, None, ALU.arith_shift_right)
                ordered()
                nc.vector.tensor_copy(hi[n], digit_t[:, :])
                ordered()

            v.wait_ge(edges_in_cols, 1)
            digits(0, src_col[:, 0:TILES])
            v.wait_ge(consts_made, 12)
            hot_batch(0, 0, 0, 0)
            hot_batch(1, 1, 1, 0)
            with v.Fori(1, HBATCHES // 2) as b:
                for half in range(2):
                    hot_batch(2 * b + half, 2 * b + half, half, 0)
            v.wait_ge(bounds_turned, 1)
            for n, to in enumerate((gmin, gmax)):
                from_tiles = banks[0:BLOCKS, n, 0:P].rearrange("b (j t) -> b j t", t=GT)
                nc.vector.tensor_reduce(to[:, :], from_tiles, AX.X, (ALU.min, ALU.max)[n])
            nc.vector.tensor_copy(floor_f[:, :], floor_i[:, :])
            ordered()
            nc.vector.tensor_copy(floor_f[:, :].rearrange("b (i k) -> b i k", k=GR)[:, :, LAST_K + 1:],
                                  floor_late[:, :, :])
            ordered()
            nc.vector.tensor_copy(gmin_i[:, :], gmin[:, :]).then_inc(bases_made, 1)
            nc.vector.tensor_tensor(gmax[:, :], gmax[:, :], gmin[:, :], ALU.subtract)
            nc.vector.tensor_scalar(floor_f[:, :], floor_f[:, :], float(PAD_DST), None, ALU.min)
            ordered()
            nc.vector.tensor_scalar(gmax[:, :], gmax[:, :], float(WIN - 1), None, ALU.is_gt)
            nc.vector.tensor_tensor(floor_f[:, :], gmin[:, :], floor_f[:, :], ALU.is_lt)
            ordered()
            nc.vector.tensor_tensor(gmax[:, :], gmax[:, :], floor_f[:, :], ALU.max)
            ordered()
            nc.vector.tensor_reduce(bad[:, 0:1], gmax[:, :], AX.X, ALU.max).then_inc(bad_counted, 1)
            v.wait_ge(bad_summed, 1)
            nc.vector.tensor_scalar(flag[:, :], banks[0:1, 2, 0:1], 0.0, None, ALU.is_gt).then_inc(flag_made, 1)
            v.wait_ge(hot_used, HBATCHES + 2)
            nc.vector.tensor_scalar(r[:, :], hist, 1.0, None, ALU.max).then_inc(degree_ready, 1)
            v.wait_ge(degree_rooted, 1)
            nc.vector.reciprocal(r[:, :], root[:, :]).then_inc(r_made, 1)
            ordered()
            v.wait_ge(x_loaded, 32)
            for c in range(NW // XCH):
                for w in range(c * XCH, c * XCH + 9):
                    nc.vector.tensor_scalar(x_all[:, w, :], x_all[:, w, :], r[:, w:w + 1], None, ALU.mult)
                ordered()
                v.wait_ge(x_scaled_act, c + 1)
                v.sem_inc(x_scaled, 1)
            v.wait_ge(bases_loaded, 16)
            nc.vector.tensor_copy(base_row_f[:, :], base_row[:, :]).then_inc(bases_float, 1)
            v.wait_ge(edges_in_cols, 2)
            nc.vector.tensor_copy(digit_t[:, :], dst_col[:, :])
            ordered()
            nc.vector.tensor_scalar(dst_rel[:, 0:TILES].bitcast(I32), digit_t[:, :], P.bit_length() - 1, None, ALU.arith_shift_right)
            ordered()
            nc.vector.tensor_copy(hi[1][:, 0:TILES], dst_rel[:, 0:TILES].bitcast(I32))
            ordered()
            nc.vector.tensor_scalar(dst_rel[:, 0:TILES].bitcast(I32), digit_t[:, :], P - 1, None, ALU.bitwise_and)
            ordered()
            nc.vector.tensor_copy(lo[1][:, 0:TILES], dst_rel[:, 0:TILES].bitcast(I32))
            ordered()
            v.wait_ge(bases_spread, 1)
            nc.vector.tensor_tensor(dst_rel[:, 0:TILES].rearrange("p (g t) -> p g t", t=GT),
                                    dst_col[:, :].rearrange("p (g t) -> p g t", t=GT),
                                    banks[:, 3, 0:GROUPS].unsqueeze(2).to_broadcast([P, GROUPS, GT]), ALU.subtract)
            ordered()
            nc.vector.tensor_copy(dst_rel[:, TILES:TILES + AHEAD * GT], dst_rel[:, 0:AHEAD * GT])
            ordered()

            def group_hot(first_tile, buf, after=0):
                rel = dst_rel[:, bass.ds(first_tile, GT)].unsqueeze(2).to_broadcast([P, GT, WIN])
                nc.vector.tensor_tensor(dst_hot[:, buf, :, :], win_iota[:, :].unsqueeze(1).to_broadcast([P, GT, WIN]),
                                        rel, ALU.is_equal).then_inc(dst_hot_made, 1)

            for c in range(NW // XCH):
                v.wait_ge(table_stored[c], 16)
                end = (c + 1) * XCH * D if c < NW // XCH - 1 else KF * ACC_N
                last = nc.vector.memset(big[:, c * XCH * D:end], 0.0)
            last.then_inc(acc_zeroed, 1)
            ordered()

            def add_group(layer, i, k):
                base = v.value_load(base_row[0:1, bass.ds(i * GR + k, 1)], min_val=0, max_val=NPAD)
                v.wait_ge(tiles_done, group_no(layer, i, k) * GT + GT + U)
                here = acc[:, :, bass.ds(base, WIN)]
                nc.vector.tensor_tensor(here, group_sum(k % 2), here, ALU.add).then_inc(groups_added, 1)

            def diagonals(m):
                for s in range(2):
                    nc.vector.tensor_scalar(r_diag[s][:, :], ident[:, :], root[:, bass.ds(2 * m + s, 1)], None,
                                            ALU.mult).then_inc(diag_ready, 1)

            def mix(m, s, sums):
                v.wait_ge(x_turned, 2 * m + s + 1)
                nc.vector.tensor_tensor(xa[s][:, :, :], turned[s][:, 0, :, :], sums, ALU.mult)
                ordered()
                nc.vector.tensor_tensor(sum_a[s][:, :, :], turned[s][:, 1, :, :], sums, ALU.add).then_inc(mixed, 1)

            def finish_sums(layer, m):
                two = bass.ds(2 * m, 2)
                if layer == 0:
                    nc.vector.scalar_tensor_tensor(pair[0], deg[:, two], 1.0, r[:, two], ALU.min, ALU.mult)
                    ordered()
                    v.wait_ge(projected, 2 * m + 2)
                    for s in range(2):
                        nc.vector.scalar_tensor_tensor(e[s][:, :], project[s], scal[:, s:s + 1], b0_s[:, :],
                                                       ALU.mult, ALU.add)
                    ordered()
                    for s in range(2):
                        nc.vector.scalar_tensor_tensor(e[s][:, :], e[s][:, :], 0.01, e[s][:, :], ALU.mult, ALU.max)
                    ordered()
                    for s in range(2):
                        nc.vector.tensor_tensor_reduce(out=out_t[s][:, :], in0=e[s][:, :], in1=e[s][:, :], scale=1.0,
                                                       scalar=0.0, op0=ALU.mult, op1=ALU.add,
                                                       accum_out=scal[:, 2 + s:3 + s])
                    ordered()
                    v.sem_inc(square_ready, 1)
                else:
                    nc.vector.tensor_scalar(pair[0], deg[:, two], 1.0, None, ALU.add)
                    ordered()
                    nc.vector.reciprocal(pair[1], pair[0])
                    ordered()
                    nc.vector.tensor_tensor(pair[2], pair[1], deg[:, two], ALU.mult)
                    ordered()
                    for s in range(2):
                        v.wait_ge(x_in[s], 16 * (node_no(1, m) + 1))
                        nc.vector.scalar_tensor_tensor(e[s][:, :], b1_s[:, :], scal[:, 4 + s:5 + s], x_t[s][:, :],
                                                       ALU.mult, ALU.add)
                    ordered()
                    v.wait_ge(projected, NW + 2 * m + 2)
                    for s in range(2):
                        nc.vector.scalar_tensor_tensor(out_t[s][:, :], project[s], scal[:, 2 + s:3 + s], e[s][:, :],
                                                       ALU.mult, ALU.add)
                    ordered()

            def moments(layer, m):
                if layer == 0:
                    v.wait_ge(norm_ready, m + 1)
                    nc.vector.tensor_scalar(pair[2], pair[2], 1e-12, None, ALU.max)
                    ordered()
                    nc.vector.reciprocal(pair[0], pair[2])
                    ordered()
                    for s in range(2):
                        nc.vector.scalar_tensor_tensor(out_t[s][:, :], e[s][:, :], scal[:, s:s + 1], x_t[s][:, :],
                                                       ALU.mult, ALU.add)
                    ordered()
                for s in range(2):
                    nc.vector.bn_stats(stats[:, s, :], out_t[s][:, :])
                ordered()
                for s in range(2):
                    nc.vector.bn_aggr(mv[:, s, :], stats[:, s, :])
                ordered()
                v.sem_inc(var_ready, 1)

            def norm(layer, m):
                v.wait_ge(var_rooted, node_no(layer, m) + 1)
                nc.vector.reciprocal(pair[3], pair[3])
                ordered()
                for s in range(2):
                    nc.vector.tensor_scalar(out_t[s][:, :], out_t[s][:, :], mv[:, s, 0:1], scal[:, 6 + s:7 + s],
                                            ALU.subtract, ALU.mult).then_inc(out_ready[s], 1)
                ordered()

            def add_hist(n):
                v.wait_ge(hot_used, n + 3)
                nc.vector.tensor_tensor(deg[:, :], hist, deg[:, :], ALU.add).then_inc(hist_added, 1)
                ordered()

            def round_(layer, i, finish):
                for k in range(GR):
                    group_hot(i * U + (k + AHEAD) * GT, (k + AHEAD) % HOTS)
                    add_group(layer, i, k)
                    ordered()
                    if layer == 0 and k % 4 == 0:
                        half = k // 4
                        hot_batch(HBATCHES + 2 * i + half + 1, 2 * i + half + 1, 1 - half, 1)
                    if layer == 0 and k % 4 == 1:
                        add_hist(HBATCHES + 2 * i + k // 4)
                    if finish and layer == 0 and k == LAST_K - 1:
                        diagonals(i - 1)
                    if finish and layer == 0 and k == LAST_K:
                        for s in range(2):
                            mix(i - 1, s, acc[:, :, bass.ds((2 * i - 2 + s) * P, P)])
                    if finish and k >= LAST_K + 2:
                        (finish_sums, moments, norm)[k - LAST_K - 2](layer, i - 1)

            v.wait_ge(w_copied, 1)
            v.wait_ge(weights_loaded, 96)
            v.wait_ge(flag_made, 1)
            disordered = v.value_load(flag[0:1, 0:1], min_val=0, max_val=1)
            with v.If(disordered == 0):
                for g in range(AHEAD):
                    group_hot(g * GT, g)
                hot_batch(HBATCHES, 0, 0, 1)
                for layer in range(2):
                    if layer == 1:
                        v.wait_ge(acc_zeroed, NW + 1)
                    round_(layer, 0, False)
                    with v.Fori(1, ROUNDS) as i:
                        round_(layer, i, True)
                    if layer == 0:
                        diagonals(ROUNDS - 1)
                        for s in range(2):
                            mix(ROUNDS - 1, s, acc[:, :, (NW - 2 + s) * P:(NW - 1 + s) * P])
                    for step in (finish_sums, moments, norm):
                        step(layer, ROUNDS - 1)
            with v.Else():
                v.sem_inc(tile_over, 1)
                with v.Fori(0, HBATCHES // 2) as b:
                    for half in range(2):
                        hot_batch(HBATCHES + 2 * b + half, 2 * b + half, half, 1)
                        add_hist(HBATCHES + 2 * b + half)
                for layer in range(2):
                    with v.Fori(0, TILES) as t:
                        n = layer * TILES + t
                        v.wait_ge(tile_over, n + 1)
                        nc.vector.tensor_copy(scal[:, 5:6], dst_col[:, bass.ds(t, 1)]).then_inc(dcol_ready, 1)
                        ordered()
                        v.wait_ge(drow_spread, n + 1)
                        nc.vector.tensor_scalar(same(ring), banks[:, 0, 0:P], scal[:, 5:6], None,
                                                ALU.is_equal).then_inc(same_ready, 1)
                        ordered()
                        nc.vector.tensor_tensor_reduce(out=ring[:, 3, 0:P], in0=same(ring), in1=lower[:, :], scale=1.0,
                                                       scalar=0.0, op0=ALU.mult, op1=ALU.add, accum_out=scal[:, 6:7])
                        ordered()
                        nc.vector.tensor_scalar(scal[:, 6:7], scal[:, 6:7], 0.0, None, ALU.is_equal)
                        nc.vector.tensor_tensor(scal[:, 7:8], scal[:, 5:6], dump_row[:, :], ALU.subtract)
                        ordered()
                        nc.vector.scalar_tensor_tensor(scal[:, 7:8], scal[:, 7:8], scal[:, 6:7], dump_row[:, :],
                                                       ALU.mult, ALU.add)
                        ordered()
                        nc.vector.tensor_copy(idx[:, 1:2], scal[:, 7:8])
                        v.wait_ge(combined, n + 1)
                        nc.vector.tensor_copy(ring[:, 1, :], banks[:, 1, 0:D])
                        ordered()
                        v.sem_inc(comb_ready, 1)
                    with v.Fori(0, ROUNDS) as m:
                        for s in range(2):
                            if layer == 0:
                                if s == 0:
                                    diagonals(m)
                                v.wait_ge(a_ready[s], m + 1)
                                mix(m, s, a_t[s][:, :, :])
                        for step in (finish_sums, moments, norm):
                            step(layer, m)

        @block.tensor
        def _(pe):
            pe.sem_inc(hot_used, 2)
            pe.sem_inc(tiles_done, U)
            pe.wait_ge(consts_made, 12)

            def turn_edges(n):
                pe.wait_ge(edges_float, n + 1)
                for b in range(BLOCKS):
                    rows = P if b < BLOCKS - 1 else LAST_BLOCK_TILES
                    last = nc.tensor.transpose(banks[:, 4 * n + b // 4, (b % 4) * P:(b % 4) * P + rows],
                                               nat[n][0:rows, b * P:(b + 1) * P], ident[0:rows, 0:rows])
                last.then_inc(edges_turned, 1)

            def hist_batch(n, half, first, last_one):
                pe.wait_ge(hot_made, n + 1)
                for t in range(HB):
                    last = nc.tensor.matmul(hist, lo_hot[half][:, :, t], hi_hot[half][:, :, t],
                                            start=first and t == 0, stop=last_one and t == HB - 1)
                last.then_inc(hot_used, 1)

            turn_edges(0)
            turn_edges(1)
            pe.wait_ge(bounds_made, 1)
            pe.wait_ge(edges_in_cols, 1)
            for n in range(2):
                last = nc.tensor.transpose(banks[0:BLOCKS, n, 0:P], bounds[:, n, :], ident[:, :])
            last.then_inc(bounds_turned, 1)
            pe.wait_ge(edges_in_cols, 2)
            hist_batch(0, 0, True, False)
            hist_batch(1, 1, False, False)
            with pe.Fori(1, HBATCHES // 2 - 1) as b:
                for half in range(2):
                    hist_batch(2 * b + half, half, False, False)
            hist_batch(HBATCHES - 2, 0, False, False)
            hist_batch(HBATCHES - 1, 1, False, True)
            pe.wait_ge(bad_counted, 1)
            nc.tensor.matmul(banks[0:1, 2, 0:1], bad[:, 0:1], ones[0:BLOCKS, 0:1],
                             start=True, stop=True).then_inc(bad_summed, 1)
            pe.wait_ge(weights_loaded, 96)
            for o, half in enumerate(xa):
                for k in range(KF):
                    last = nc.tensor.transpose(banks[:, 0, k * D + o * P:k * D + (o + 1) * P], half[:, k, :], ident[:, :])
            last.then_inc(w_turned, 1)
            pe.wait_ge(bases_float, 1)
            nc.tensor.matmul(banks[:, 3, 0:GROUPS], ones[0:1, :], base_row_f[:, 0:GROUPS],
                             start=True, stop=True).then_inc(bases_spread, 1)

            def turn_x(m, s):
                if s == 0:
                    pe.wait_ge(diag_ready, 2 * m + 2)
                pe.wait_ge(x_in[s], 16 * (m + 1))
                for k in range(KF):
                    nc.tensor.transpose(turned[s][:, 0, k, :], x_t[s][:, k * P:(k + 1) * P], ident[:, :])
                for k in range(KF):
                    last = nc.tensor.matmul(turned[s][:, 1, k, :], x_t[s][:, k * P:(k + 1) * P], r_diag[s][:, :],
                                            start=True, stop=True)
                last.then_inc(x_turned, 1)

            def products(layer, m, s, taken):
                if layer == 0:
                    pe.wait_ge(mixed, 2 * m + 2 if s == 1 else 2 * m + 1)
                    parts = [(xa[s][:, k, :], w2_s[:, k, :]) for k in range(KF)]
                    parts += [(sum_a[s][:, k, :], w1_s[:, k, :]) for k in range(KF)]
                else:
                    pe.wait_ge(a_ready[s], taken + 1)
                    parts = [(a_t[s][:, k, :], wt_s[:, k, :]) for k in range(KF)]
                for k, (left, right) in enumerate(parts):
                    last = nc.tensor.matmul(project[s], left, right, start=k == 0, stop=k == len(parts) - 1)
                last.then_inc(projected, 1)

            def dst_hist(n, half):
                pe.wait_ge(hist_added, n - HBATCHES + 1)
                hist_batch(n, half, True, True)

            def round_(layer, i, finish):
                for k in range(GR):
                    if layer == 0 and k in (0, GR // 2):
                        half = k // (GR // 2)
                        dst_hist(HBATCHES + 2 * i + half, half)
                    pe.wait_ge(dst_hot_made, group_no(layer, i, k) + 1)
                    pe.wait_ge(groups_added, group_no(layer, i, k) + 1)
                    for j in range(GT):
                        u = k * GT + j
                        pe.wait_ge(rows_in[u], 16 * (layer * ROUNDS + i + 1))
                        for f in range(KF):
                            last = nc.tensor.matmul(group_sum(k % 2)[:, f, :], ring[:, u, f * P:(f + 1) * P],
                                                    dst_hot[:, k % HOTS, j, :], start=j == 0, stop=j == GT - 1)
                        last.then_inc(tiles_done, 1)
                    if finish and layer == 0 and k == LAST_K:
                        for s in range(2):
                            turn_x(i - 1, s)
                    if finish and k == LAST_K + 1:
                        for s in range(2):
                            products(layer, i - 1, s, i - 1)

            pe.wait_ge(r_made, 1)
            pe.wait_ge(w_copied, 1)
            pe.wait_ge(flag_made, 1)
            disordered = pe.value_load(flag[0:1, 0:1], min_val=0, max_val=1)
            with pe.If(disordered == 0):
                for layer in range(2):
                    round_(layer, 0, False)
                    with pe.Fori(1, ROUNDS) as i:
                        round_(layer, i, True)
                    if layer == 0:
                        for s in range(2):
                            turn_x(ROUNDS - 1, s)
                    for s in range(2):
                        products(layer, ROUNDS - 1, s, ROUNDS - 1)
            with pe.Else():
                with pe.Fori(0, HBATCHES // 2) as b:
                    for half in range(2):
                        dst_hist(HBATCHES + 2 * b + half, half)
                for layer in range(2):
                    with pe.Fori(0, TILES) as t:
                        n = layer * TILES + t
                        pe.wait_ge(dcol_ready, n + 1)
                        nc.tensor.matmul(banks[:, 0, 0:P], scal[:, 5:6].to_broadcast([P, P]), ident[:, :],
                                         start=True, stop=True).then_inc(drow_spread, 1)
                        pe.wait_ge(same_ready, n + 1)
                        pe.wait_ge(row_in, 16 * (n + 1))
                        nc.tensor.matmul(banks[:, 1, 0:D], same(ring), ring[:, 0, :],
                                         start=True, stop=True).then_inc(combined, 1)
                    with pe.Fori(0, ROUNDS) as m:
                        for s in range(2):
                            pe.wait_ge(sums_in, 16 * (layer * NW + 2 * m + s + 1))
                            for k in range(KF):
                                last = nc.tensor.transpose(banks[:, 0, k * P:(k + 1) * P],
                                                           sums_t[:, k * P:(k + 1) * P], ident[:, :])
                            last.then_inc(sums_turned, 1)
                            if layer == 0:
                                turn_x(m, s)
                            products(layer, m, s, node_no(layer, m))


def same(ring):
    return ring[:, 2, 0:P]


_INS = ["x", "src", "dst", "L0_gnn_W1", "L0_gnn_W2", "L0_gnn_b", "L1_gnn_W", "L1_gnn_b"]


def kernel(**inputs):
    import numpy as np
    import concourse.bacc as bacc
    from concourse import mybir as mb
    from concourse.bass_utils import run_bass_kernel_spmd

    nc = bacc.Bacc("TRN2", target_bir_lowering=False, num_devices=1)
    arrays, args = {}, []
    for name in _INS:
        a = np.ascontiguousarray(inputs[name])
        arrays[f"in_{name}"] = a
        args.append(nc.dram_tensor(f"in_{name}", a.shape, mb.dt.from_np(a.dtype), kind="ExternalInput").ap())
    result = nc.dram_tensor("result", (NODES, D), mb.dt.float32, kind="ExternalOutput").ap()
    gnn(nc, *args, result)
    r = run_bass_kernel_spmd(nc, [arrays], core_ids=[0])
    return r.results[0]["result"]
```

```python
import concourse.bass as bass
from concourse import mybir
from contextlib import ExitStack

F32, BF16, I32 = mybir.dt.float32, mybir.dt.bfloat16, mybir.dt.int32
ALU = mybir.AluOpType
ACT = mybir.ActivationFunctionType
AX = mybir.AxisListType

P = 128
D = 256
KF = D // P
NODES = 12500
EDGES = 200000
NW = -(-NODES // P)
NPAD = NW * P
LAST_ROWS = NODES - (NW - 1) * P
ROUNDS = NW // 2
U = 32
TILES = ROUNDS * U
GT = 4
GR = U // GT
GROUPS = TILES // GT
WIN = 64
ACC_N = NPAD + WIN
BLOCKS = -(-TILES // P)
FULL_TILES = EDGES // P
LAST_EDGES = EDGES - FULL_TILES * P
LAST_BLOCK_TILES = TILES - (BLOCKS - 1) * P
PAD_SRC = NPAD - 1
PAD_DST = NODES
HB = 16
HBATCHES = TILES // HB
SB = 4
STEP_BATCHES = 72
STEP_TILES = STEP_BATCHES * SB
SRC_BATCHES = (TILES - STEP_TILES) // HB
SPANS = 8
HI = NW
LAST_K = 2
AHEAD = 3
HOTS = 4
QT = U // 4
FINAL = -(-EDGES // P) - (ROUNDS - 1) * U
X_CHUNKS = [(w, min(w + 14, NW)) for w in range(-8, NW, 14)]
X_CHUNKS[0] = (0, X_CHUNKS[0][1])
RAW = 7 * GT
RAW_EARLY = [u for u in range(RAW) if 3 <= u < 13 or 20 <= u < 26]
RAW_LATE = [u for u in range(RAW) if u not in RAW_EARLY]
RAW_FIRST = 3
FIRST_GROUPS = 3
DUMP = NPAD


def gnn(nc, x, src, dst, w1, w2, b0, wl, b1, out):
    table = [nc.dram_tensor("scaled_x", (NPAD, D), F32, kind="Internal").ap(),
             nc.dram_tensor("x1", (NPAD, D), F32, kind="Internal").ap()]
    r_dram = nc.dram_tensor("r_table", (NPAD, 1), F32, kind="Internal").ap()
    base_dram = nc.dram_tensor("group_bases", (BLOCKS * U,), I32, kind="Internal").ap()
    sums_dram = [nc.dram_tensor(f"sums{n}", (NPAD + P, D), F32, kind="Internal").ap() for n in range(2)]

    with ExitStack() as ctx:
        def sb(name, shape, dt=F32):
            return ctx.enter_context(nc.sbuf_tensor(name, shape, dt))

        def sem(name):
            return ctx.enter_context(nc.semaphore(name))

        big = sb("big", [P, KF * ACC_N])
        acc = big[:, :].rearrange("p (k n) -> p k n", k=KF)
        x_all = big[:, 0:NW * D].rearrange("p (w f) -> p w f", w=NW)
        ring = sb("ring", [P, U, D])
        ring_flat = ring[:, :, :].rearrange("p u f -> p (u f)")
        nat = [ring_flat[:, n * BLOCKS * P:(n + 1) * BLOCKS * P] for n in range(2)]
        nat_i = [ring_flat[:, (2 + n) * BLOCKS * P:(3 + n) * BLOCKS * P].bitcast(I32) for n in range(2)]
        src_col = sb("src_col", [P, TILES + U], I32)
        dst_col = sb("dst_col", [P, TILES])
        dst_rel = sb("dst_rel", [P, TILES + AHEAD * GT])
        src_digits = ring_flat[:, 2 * BLOCKS * P:3 * BLOCKS * P].bitcast(BF16)
        lo = [src_digits[:, 0:TILES], sb("dst_lo", [P, TILES + HB], BF16)[:, :]]
        hi = [src_digits[:, TILES:2 * TILES], sb("dst_hi", [P, TILES + HB], BF16)[:, :]]
        count_to = sb("count_to", [P, P, HB], BF16)
        hot = sb("hot", [P, 2, P + HI, HB], BF16)
        lo_hot = [hot[:, n, 0:P, :] for n in range(2)]
        hi_hot = [hot[:, n, P:P + HI, :] for n in range(2)]
        steps = ring_flat[:, 4 * BLOCKS * P:].bitcast(BF16)[:, 0:3 * SB * (P + HI)].rearrange(
            "p (n t j) -> p n t j", n=3, t=SB)
        step_digits = nat[0][:, 0:2 * STEP_TILES].rearrange("p (d t) -> p d t", d=2)
        digit_t = hot[:, :, :, :].rearrange("p a b c -> p (a b c)")[:, 0:2 * TILES].bitcast(I32)
        win_iota = sb("win_iota", [P, WIN])
        dst_hot = sb("dst_hot", [P, HOTS, GT, WIN])
        idx = sb("idx", [P, U], I32)
        ident = sb("ident", [P, P])
        lower = sb("lower", [P, P])
        between = sb("between", [P, P])
        ones = sb("ones", [P, P])
        zeros = sb("zeros", [P, D])
        dump_row = sb("dump_row", [P, 1])
        epsilon = sb("epsilon", [P, 1])
        bounds = sb("bounds", [P, 2, BLOCKS])
        gmin = sb("gmin", [BLOCKS, U])
        gmax = sb("gmax", [BLOCKS, U])
        floor_i = sb("floor_i", [BLOCKS, U], I32)
        floor_late = sb("floor_late", [BLOCKS, U // GR, GR - LAST_K - 1], I32)
        floor_f = sb("floor_f", [BLOCKS, U])
        gmin_i = sb("gmin_i", [BLOCKS, U], I32)
        bad = sb("bad", [BLOCKS, 4])
        flag = sb("flag", [1, 1], I32)
        base_row = sb("base_row", [1, BLOCKS * U], I32)
        base_row_f = dst_hot[0:1, 0:2, :, :].rearrange("p a b c -> p (a b c)")[:, 0:BLOCKS * U]
        r = sb("r", [P, NW])
        r_edge = sb("r_edge", [P, RAW])
        root = sb("root", [P, NW])
        r_diag = [sb(f"r_diag{n}", [P, P]) for n in range(2)]
        columns = r_diag[0]
        deg = sb("deg", [P, NW])
        w1_s = sb("w1_s", [P, KF, D])
        w2_s = sb("w2_s", [P, KF, D])
        wt_s = sb("wt_s", [P, KF, D])
        b0_s = sb("b0_s", [P, D])
        b1_s = sb("b1_s", [P, D])
        x_t = [sb(f"x_t{n}", [P, D]) for n in range(2)]
        a_t = [sb(f"a_t{n}", [P, KF, P]) for n in range(2)]
        out_t = [sb(f"out_t{n}", [P, D]) for n in range(2)]
        sums_t = sb("sums_t", [P, D])
        sum_a = a_t
        xa = [sb(f"xa{n}", [P, KF, P]) for n in range(2)]
        e = [sb(f"e{n}", [P, D]) for n in range(2)]
        step_rows = [e[n][:, 0:HI] for n in range(2)]
        r_rows = e[0][0:NW, 0:P]
        scal = sb("scal", [P, 8])
        pair = [scal[:, 2 * n:2 * n + 2] for n in range(4)]
        stats = sb("stats", [P, 2, 6])
        mv = sb("mv", [P, 2, 2])

        banks = ctx.enter_context(nc.psum_tensor("banks", [P, 8, 512], F32))

        def group_sum(buf):
            return banks[:, 2 * buf:2 * buf + 2, 0:WIN]

        hist = banks[:, 4, 0:HI]
        step_sums = banks[:, 3, 0:HI]
        turned = [banks[:, 5 + s, :].rearrange("p (a k n) -> p a k n", a=2, k=KF) for s in range(2)]
        project = [banks[:, 7, 0:D], banks[:, 5, 0:D]]

        consts_made = sem("consts_made")
        edges_loaded = [sem(f"edges_loaded{n}") for n in range(2)]
        edges_padded = sem("edges_padded")
        weights_loaded = sem("weights_loaded")
        x_loaded = sem("x_loaded")
        x_padded = sem("x_padded")
        edges_float = sem("edges_float")
        edges_turned = sem("edges_turned")
        edges_in_cols = sem("edges_in_cols")
        bounds_made = sem("bounds_made")
        bounds_turned = sem("bounds_turned")
        bounds_read = sem("bounds_read")
        bad_counted = sem("bad_counted")
        bad_summed = sem("bad_summed")
        bases_made = sem("bases_made")
        bases_stored = sem("bases_stored")
        bases_loaded = sem("bases_loaded")
        bases_float = sem("bases_float")
        bases_spread = sem("bases_spread")
        flag_made = sem("flag_made")
        w_turned = sem("w_turned")
        w_copied = sem("w_copied")
        hot_made = sem("hot_made")
        hot_used = sem("hot_used")
        step_digits_made = sem("step_digits_made")
        steps_made = sem("steps_made")
        steps_used = sem("steps_used")
        step_diffs_made = sem("step_diffs_made")
        counts_whole = sem("counts_whole")
        degree_ready = sem("degree_ready")
        degree_rooted = sem("degree_rooted")
        r_made = sem("r_made")
        r_turned = sem("r_turned")
        r_rows_made = sem("r_rows_made")
        r_stored = sem("r_stored")
        raw_turn = sem("raw_turn")
        r_edges_in = [sem(f"r_edges_in{n}") for n in range(2)]
        x_scaled_act = sem("x_scaled_act")
        x_scaled = sem("x_scaled")
        table_stored = [sem(f"table_stored{c}") for c in range(len(X_CHUNKS))]
        acc_zeroed_act = sem("acc_zeroed_act")
        acc_zeroed = sem("acc_zeroed")
        idx_ready = sem("idx_ready")
        rows_in = [sem(f"rows_in{u}") for u in range(U)]
        gather_turn = sem("gather_turn")
        dst_hot_made = sem("dst_hot_made")
        tiles_done = sem("tiles_done")
        groups_added = sem("groups_added")
        act_turn = sem("act_turn")
        x_in = [sem(f"x_in{n}") for n in range(2)]
        sums_in = sem("sums_in")
        stored = [sem(f"stored{n}") for n in range(2)]
        out_ready = [sem(f"out_ready{n}") for n in range(2)]
        a_ready = [sem(f"a_ready{n}") for n in range(2)]
        diag_ready = sem("diag_ready")
        x_turned = sem("x_turned")
        sums_turned = sem("sums_turned")
        mixed = sem("mixed")
        hist_added = sem("hist_added")
        projected = sem("projected")
        square_ready = sem("square_ready")
        norm_ready = sem("norm_ready")
        var_ready = sem("var_ready")
        var_rooted = sem("var_rooted")
        table1_whole = sem("table1_whole")
        dcol_ready = sem("dcol_ready")
        drow_spread = sem("drow_spread")
        same_ready = sem("same_ready")
        to_ready = sem("to_ready")
        combined = sem("combined")
        comb_ready = sem("comb_ready")
        one_idx_ready = sem("one_idx_ready")
        row_in = sem("row_in")
        row_added = sem("row_added")
        tile_over = sem("tile_over")
        sums_zeroed = sem("sums_zeroed")

        block = ctx.enter_context(nc.Block())

        def group_no(layer, i, k):
            return layer * GROUPS + i * GR + k

        def node_no(layer, m):
            return layer * ROUNDS + m

        @block.sync
        def _(sp):
            for s in range(2):
                sp.sem_inc(stored[s], 16)
            sp.wait_ge(edges_padded, 1)
            for n, edges in enumerate((src, dst)):
                whole = (BLOCKS - 1) * P
                v = nat_i[n].rearrange("p (b e) -> p b e", b=BLOCKS)
                sp.dma_start(v[:, 0:BLOCKS - 1, :],
                             edges[0:whole * P].rearrange("(b p e) -> p b e", p=P, e=P)).then_inc(edges_loaded[n], 16)
                sp.dma_start(v[0:FULL_TILES - whole, BLOCKS - 1, :],
                             edges[whole * P:FULL_TILES * P].rearrange("(p e) -> p e", e=P)).then_inc(edges_loaded[n], 16)
                sp.dma_start(v[FULL_TILES - whole:FULL_TILES - whole + 1, BLOCKS - 1, 0:LAST_EDGES],
                             edges[FULL_TILES * P:EDGES].rearrange("(p e) -> p e", p=1)).then_inc(edges_loaded[n], 16)
            sp.wait_ge(x_padded, 1)
            x_rows = x[0:(NW - 1) * P, :].rearrange("(w p) f -> p w f", p=P)
            sp.dma_start(x_all[:, 0:NW - 1, :], x_rows).then_inc(x_loaded, 16)
            sp.dma_start(x_all[0:LAST_ROWS, NW - 1, :], x[(NW - 1) * P:NODES, :]).then_inc(x_loaded, 16)
            sp.dma_start(w1_s[:, :, :], w1.rearrange("(k p) n -> p k n", p=P)).then_inc(weights_loaded, 16)
            sp.dma_start(w2_s[:, :, :], w2.rearrange("(k p) n -> p k n", p=P)).then_inc(weights_loaded, 16)
            sp.dma_start(xa[0][:, :, :].rearrange("p a b -> p (a b)"), wl[0:P, :]).then_inc(weights_loaded, 16)
            sp.dma_start(xa[1][:, :, :].rearrange("p a b -> p (a b)"), wl[P:D, :]).then_inc(weights_loaded, 16)
            sp.dma_start(b0_s[:, :], b0.rearrange("(a n) -> a n", a=1).to_broadcast([P, D])).then_inc(weights_loaded, 16)
            sp.dma_start(b1_s[:, :], b1.rearrange("(a n) -> a n", a=1).to_broadcast([P, D])).then_inc(weights_loaded, 16)
            sp.wait_ge(bases_made, 1)
            sp.dma_start(base_dram.rearrange("(b j) -> b j", b=BLOCKS), gmin_i[:, :]).then_inc(bases_stored, 16)
            sp.wait_ge(bases_stored, 16)
            sp.dma_start(base_row[:, :], base_dram.rearrange("(a n) -> a n", a=1)).then_inc(bases_loaded, 16)
            sp.wait_ge(r_rows_made, 1)
            sp.dma_start(r_dram.rearrange("(w p) a -> w (p a)", p=P), r_rows).then_inc(r_stored, 16)
            for c, (first, end) in enumerate(X_CHUNKS):
                sp.wait_ge(x_scaled, c + 1)
                sp.dma_start(table[0][first * P:end * P, :].rearrange("(w p) f -> p w f", p=P),
                             x_all[:, first:end, :]).then_inc(table_stored[c], 16)

            def load_x(layer, m, w, s):
                if layer == 1:
                    rows = table[1][bass.ds(w * P, P), :]
                    sp.dma_start(x_t[s][:, :], rows).then_inc(x_in[s], 16)
                elif isinstance(w, int) and w == NW - 1:
                    sp.dma_start(x_t[s][0:LAST_ROWS, :], x[w * P:NODES, :]).then_inc(x_in[s], 16)
                else:
                    sp.dma_start(x_t[s][:, :], x[bass.ds(w * P, P), :]).then_inc(x_in[s], 16)

            def store(layer, m, w, s):
                sp.wait_ge(out_ready[s], node_no(layer, m) + 1)
                if layer == 0:
                    sp.dma_start(table[1][bass.ds(w * P, P), :], out_t[s][:, :]).then_inc(stored[s], 16)
                elif isinstance(w, int) and w == NW - 1:
                    sp.dma_start(out[w * P:NODES, :], out_t[s][0:LAST_ROWS, :]).then_inc(stored[s], 16)
                else:
                    sp.dma_start(out[bass.ds(w * P, P), :], out_t[s][:, :]).then_inc(stored[s], 16)

            def next_pair(layer, m):
                sp.wait_ge(var_ready, node_no(layer, m) + 1)
                for s in range(2):
                    load_x(layer, m + 1, 2 * m + 2 + s, s)
                for s in range(2):
                    store(layer, m, 2 * m + s, s)

            def layer_end(layer):
                for s in range(2):
                    sp.wait_ge(stored[s], 16 * ((layer + 1) * ROUNDS + 1))
                if layer == 0:
                    sp.sem_inc(table1_whole, 1)

            def sum_rows(layer, m, s, w):
                if not (layer == 0 and s == 0 and isinstance(m, int)):
                    sp.wait_ge(sums_turned, layer * NW + 2 * m + s)
                sp.dma_start(sums_t[:, :], sums_dram[layer][bass.ds(w * P, P), :]).then_inc(sums_in, 16)

            sp.wait_ge(flag_made, 1)
            disordered = sp.value_load(flag[0:1, 0:1], min_val=0, max_val=1)
            with sp.If(disordered == 0):
                for layer in range(2):
                    for s in range(2):
                        load_x(layer, 0, s, s)
                    with sp.Fori(0, ROUNDS - 2) as m:
                        next_pair(layer, m)
                    next_pair(layer, ROUNDS - 2)
                    for s in range(2):
                        store(layer, ROUNDS - 1, NW - 2 + s, s)
                    layer_end(layer)
            with sp.Else():
                sp.wait_ge(acc_zeroed, 1)
                for n in range(2):
                    sp.dma_start(sums_dram[n][0:NPAD, :].rearrange("(p w) f -> p (w f)", p=P),
                                 big[:, 0:NW * D]).then_inc(sums_zeroed, 16)
                    sp.dma_start(sums_dram[n][NPAD:NPAD + P, :], zeros[:, :]).then_inc(sums_zeroed, 16)
                for layer in range(2):
                    sp.wait_ge(tile_over, (layer + 1) * TILES + 1)
                    for s in range(2):
                        load_x(layer, 0, s, s)
                    for s in range(2):
                        sum_rows(layer, 0, s, s)
                    with sp.Fori(0, ROUNDS - 2) as m:
                        next_pair(layer, m)
                        for s in range(2):
                            sum_rows(layer, m + 1, s, 2 * m + 2 + s)
                    next_pair(layer, ROUNDS - 2)
                    for s in range(2):
                        sum_rows(layer, ROUNDS - 1, s, NW - 2 + s)
                    for s in range(2):
                        store(layer, ROUNDS - 1, NW - 2 + s, s)
                    layer_end(layer)

        @block.gpsimd
        def _(g):
            nc.gpsimd.iota(count_to[:, :, :], pattern=[[1, P], [0, HB]], base=0, channel_multiplier=0,
                           allow_small_or_imprecise_dtypes=True).then_inc(consts_made, 1)
            nc.gpsimd.iota(win_iota[:, :], pattern=[[1, WIN]], base=0, channel_multiplier=0,
                           allow_small_or_imprecise_dtypes=True).then_inc(consts_made, 1)
            nc.gpsimd.iota(floor_i[:, :], pattern=[[2 * P, U // GR], [0, GR]], base=-2 * P,
                           channel_multiplier=2 * P * (U // GR)).then_inc(consts_made, 1)
            nc.gpsimd.iota(floor_late[:, :, :], pattern=[[2 * P, U // GR], [0, GR - LAST_K - 1]], base=0,
                           channel_multiplier=2 * P * (U // GR)).then_inc(consts_made, 1)
            nc.gpsimd.iota(dump_row[:, :], pattern=[[0, 1]], base=DUMP, channel_multiplier=1,
                           allow_small_or_imprecise_dtypes=True).then_inc(consts_made, 1)
            nc.gpsimd.memset(ident[:, :], 0.0).then_inc(consts_made, 1)
            nc.gpsimd.memset(lower[:, :], 1.0).then_inc(consts_made, 1)
            nc.gpsimd.memset(ones[:, :], 1.0).then_inc(consts_made, 1)
            nc.gpsimd.memset(zeros[:, :], 0.0).then_inc(consts_made, 1)
            nc.gpsimd.memset(epsilon[:, :], 1e-5).then_inc(consts_made, 1)
            nc.gpsimd.iota(columns[:, :], pattern=[[1, P]], base=0, channel_multiplier=0,
                           allow_small_or_imprecise_dtypes=True).then_inc(consts_made, 1)
            nc.gpsimd.memset(between[:, :], 0.0).then_inc(consts_made, 1)
            g.wait_ge(consts_made, 12)
            nc.gpsimd.affine_select(out=ident[:, :], in_=ident[:, :], compare_op=ALU.not_equal, fill=1.0, base=0,
                                    pattern=[[-1, P]], channel_multiplier=1).then_inc(consts_made, 1)
            nc.gpsimd.affine_select(out=lower[:, :], in_=lower[:, :], compare_op=ALU.is_gt, fill=0.0, base=0,
                                    pattern=[[-1, P]], channel_multiplier=1).then_inc(consts_made, 1)
            for n, (value, offset) in enumerate(((0.25, 0), (-0.25, 1), (0.25, 1 - P))):
                g.wait_ge(consts_made, 14 + n)
                nc.gpsimd.affine_select(out=between[:, :], in_=between[:, :], compare_op=ALU.not_equal, fill=value,
                                        base=offset, pattern=[[-1, P]], channel_multiplier=1).then_inc(consts_made, 1)

            def gather_quarter(layer, i, q, end=U, begin=0):
                g.wait_ge(idx_ready, (layer * ROUNDS + i) * 4 + q + 1)
                g.sem_inc(gather_turn, 1)
                for u in range(max(q * QT, begin), min((q + 1) * QT, end)):
                    g.indirect_dma_start(ring[:, u, :], None, table[layer],
                                         bass.IndirectOffsetOnAxis(ap=idx[:, u:u + 1], axis=0)).then_inc(rows_in[u], 16)

            def gather_raw(u):
                g.indirect_dma_start(ring[:, u, :], None, x,
                                     bass.IndirectOffsetOnAxis(ap=idx[:, u:u + 1], axis=0)).then_inc(rows_in[u], 16)

            def gather_r(u, n):
                g.indirect_dma_start(r_edge[:, u:u + 1], None, r_dram,
                                     bass.IndirectOffsetOnAxis(ap=idx[:, u:u + 1], axis=0)).then_inc(r_edges_in[n], 16)

            g.wait_ge(idx_ready, 4)
            g.wait_ge(step_digits_made, 1)
            for u in RAW_EARLY:
                gather_raw(u)
            g.wait_ge(r_made, 1)
            for u in RAW_LATE[:RAW_FIRST]:
                gather_raw(u)
            g.wait_ge(r_stored, 16)
            for u in RAW_LATE[:RAW_FIRST] + RAW_EARLY:
                gather_r(u, 0)
            for u in RAW_LATE[RAW_FIRST:]:
                gather_raw(u)
            for u in RAW_LATE[RAW_FIRST:]:
                gather_r(u, 1)
            for c in range(len(X_CHUNKS)):
                g.wait_ge(table_stored[c], 16)
            g.wait_ge(flag_made, 1)
            disordered = g.value_load(flag[0:1, 0:1], min_val=0, max_val=1)
            with g.If(disordered == 0):
                for layer in range(2):
                    if layer == 1:
                        g.wait_ge(table1_whole, 1)
                    for q in range(4):
                        gather_quarter(layer, 0, q, begin=RAW if layer == 0 else 0)
                    with g.Fori(1, ROUNDS - 1) as i:
                        for q in range(4):
                            gather_quarter(layer, i, q)
                    for q in range(4):
                        gather_quarter(layer, ROUNDS - 1, q, FINAL)
            with g.Else():
                g.wait_ge(sums_zeroed, 64)
                for u in range(RAW):
                    g.wait_ge(rows_in[u], 16)
                g.wait_ge(r_edges_in[0], 16 * (RAW_FIRST + len(RAW_EARLY)))
                g.wait_ge(r_edges_in[1], 16 * (len(RAW_LATE) - RAW_FIRST))
                g.sem_inc(tile_over, 1)
                for layer in range(2):
                    if layer == 1:
                        g.wait_ge(table1_whole, 1)
                    with g.Fori(0, TILES) as t:
                        g.wait_ge(one_idx_ready, layer * TILES + t + 1)
                        g.sem_inc(gather_turn, 1)
                        g.indirect_dma_start(ring[:, 0, :], None, table[layer],
                                             bass.IndirectOffsetOnAxis(ap=idx[:, 0:1], axis=0)).then_inc(row_in, 16)
                        g.wait_ge(comb_ready, layer * TILES + t + 1)
                        g.sem_inc(gather_turn, 1)
                        g.indirect_dma_start(sums_dram[layer],
                                             bass.IndirectOffsetOnAxis(ap=idx[:, 1:2], axis=0), ring[:, 1, :], None,
                                             compute_op=ALU.add).then_inc(row_added, 16)
                        g.wait_ge(row_added, 16 * (layer * TILES + t + 1))
                        g.sem_inc(tile_over, 1)

        @block.scalar
        def _(act):
            for n in range(2):
                act.wait_ge(edges_turned, 1 + n)
                cols = banks[:, 4 * n:4 * n + 4, :].rearrange("p a b -> p (a b)")[:, 0:TILES]
                nc.scalar.copy((src_col[:, 0:TILES], dst_col[:, :])[n], cols).then_inc(edges_in_cols, 1)
            act.wait_ge(consts_made, 17)
            act.drain()
            nc.scalar.copy(src_col[:, TILES:TILES + U], src_col[:, 0:U])
            nc.scalar.copy(idx[:, :], src_col[:, 0:U]).then_inc(idx_ready, 4)

            def step_batch(n, third):
                act.wait_ge(steps_used, n + 1)
                act.sem_inc(act_turn, 1)
                for t in range(SB):
                    for digit, (first, size) in enumerate(((0, P), (P, HI))):
                        last = nc.scalar.activation(steps[:, third, t, first:first + size], columns[:, 0:size], ACT.Sign,
                                                    bias=step_digits[:, digit, bass.ds(n * SB + t, 1)], scale=-1.0)
                last.then_inc(steps_made, 1)

            act.wait_ge(step_digits_made, 1)
            with act.Fori(0, STEP_BATCHES // 3) as b:
                for third in range(3):
                    step_batch(3 * b + third, third)
            act.wait_ge(degree_ready, 1)
            nc.scalar.activation(root[:, :], r[:, :], ACT.Sqrt).then_inc(degree_rooted, 1)
            act.wait_ge(r_turned, 1)
            nc.scalar.copy(r_rows, banks[0:NW, 2, 0:P]).then_inc(r_rows_made, 1)
            act.wait_ge(x_loaded, 32)
            for first, end in X_CHUNKS:
                for w in range(end - (end - first) * 2 // 5, end):
                    last = nc.scalar.activation(x_all[:, w, :], x_all[:, w, :], ACT.Copy, scale=r[:, w:w + 1])
                last.then_inc(x_scaled_act, 1)
            act.wait_ge(w_turned, 1)
            nc.scalar.copy(wt_s[:, :, :], banks[:, 0, :].rearrange("p (k o) -> p k o", k=KF)).then_inc(w_copied, 1)
            for c, (first, end) in enumerate(X_CHUNKS):
                if c % 2 == 1:
                    act.wait_ge(table_stored[c], 16)
                    whole = big[:, first * D:end * D].rearrange("p (w f) -> p w f", f=D)
                    last = nc.scalar.copy(whole, zeros[:, :].unsqueeze(1).to_broadcast([P, end - first, D]))
            last.then_inc(acc_zeroed_act, 1)

            def refill(layer, i, q):
                act.wait_ge(tiles_done, (layer * ROUNDS + i) * U + q * QT + QT + U)
                act.sem_inc(act_turn, 1)
                nc.scalar.copy(idx[:, q * QT:(q + 1) * QT],
                               src_col[:, bass.ds(i * U + U + q * QT, QT)]).then_inc(idx_ready, 1)

            def clear_sums(m, s):
                act.wait_ge(mixed, 2 * m + s + 1)
                act.sem_inc(act_turn, 1)
                nc.scalar.copy(acc[:, :, bass.ds((2 * m + s) * P, P)],
                               zeros[:, :].rearrange("p (k n) -> p k n", k=KF)).then_inc(acc_zeroed, 1)

            def take_sums(m, s, added):
                act.wait_ge(groups_added, added + 2)
                act.sem_inc(act_turn, 1)
                nc.scalar.copy(a_t[s][:, :, :], acc[:, :, bass.ds((2 * m + s) * P, P)]).then_inc(a_ready[s], 1)

            def roots(layer, m):
                if layer == 0:
                    act.wait_ge(square_ready, m + 1)
                    nc.scalar.activation(pair[2], pair[1], ACT.Sqrt).then_inc(norm_ready, 1)
                act.wait_ge(var_ready, node_no(layer, m) + 1)
                nc.scalar.activation(pair[3], mv[:, :, 1], ACT.Sqrt, bias=epsilon[:, 0:1]).then_inc(var_rooted, 1)

            def round_(layer, i, finish):
                for q in range(4):
                    for s in range(2 if finish and q == 1 else 0):
                        if layer == 0:
                            clear_sums(i - 1, s)
                        else:
                            take_sums(i - 1, s, group_no(layer, i, LAST_K + 1))
                    refill(layer, i, q)
                    if finish and q == 2:
                        roots(layer, i - 1)

            act.wait_ge(flag_made, 1)
            disordered = act.value_load(flag[0:1, 0:1], min_val=0, max_val=1)
            with act.If(disordered == 0):
                for layer in range(2):
                    round_(layer, 0, False)
                    with act.Fori(1, ROUNDS) as i:
                        round_(layer, i, True)
                    for s in range(2):
                        if layer == 0:
                            clear_sums(ROUNDS - 1, s)
                        else:
                            take_sums(ROUNDS - 1, s, (layer + 1) * GROUPS)
                    roots(layer, ROUNDS - 1)
            with act.Else():
                for layer in range(2):
                    with act.Fori(0, TILES) as t:
                        act.wait_ge(tile_over, layer * TILES + t + 1)
                        act.sem_inc(act_turn, 1)
                        nc.scalar.copy(idx[:, 0:1], src_col[:, bass.ds(t, 1)]).then_inc(one_idx_ready, 1)
                    with act.Fori(0, ROUNDS) as m:
                        for s in range(2):
                            act.wait_ge(sums_turned, layer * NW + 2 * m + s + 1)
                            nc.scalar.copy(a_t[s][:, :, :],
                                           banks[:, 0, 0:D].rearrange("p (k n) -> p k n", k=KF)).then_inc(a_ready[s], 1)
                        roots(layer, m)

        @block.vector
        def _(v):
            def ordered():
                v.drain()

            def hot_batch(n, batch, half, which):
                v.wait_ge(hot_used, n + 1)
                for digit, hots, size in ((lo, lo_hot, P), (hi, hi_hot, HI)):
                    vals = digit[which][:, bass.ds(batch * HB, HB)].unsqueeze(1).to_broadcast([P, size, HB])
                    last = nc.vector.tensor_tensor(hots[half], vals, count_to[:, 0:size, :], ALU.is_equal)
                last.then_inc(hot_made, 1)

            v.sem_inc(groups_added, 2)
            v.sem_inc(hist_added, 1)
            last_block = (BLOCKS - 1) * P
            nc.vector.memset(nat_i[0][:, last_block:last_block + P], PAD_SRC)
            nc.vector.memset(nat_i[1][:, last_block:last_block + P], PAD_DST).then_inc(edges_padded, 1)
            nc.vector.memset(x_all[:, NW - 1, :], 0.0).then_inc(x_padded, 1)
            nc.vector.memset(deg[:, :], 0.0)
            for digit in (lo[1], hi[1]):
                nc.vector.memset(digit[:, TILES:TILES + HB], 0.0)
            for n in range(2):
                v.wait_ge(edges_loaded[n], 48)
                nc.vector.tensor_copy(nat[n], nat_i[n]).then_inc(edges_float, 1)
            ordered()
            by_tile = nat[1].rearrange("p (b e) -> p b e", b=BLOCKS)
            nc.vector.tensor_reduce(bounds[:, 0, :], by_tile, AX.X, ALU.min)
            nc.vector.tensor_reduce(bounds[:, 1, :], by_tile, AX.X, ALU.max).then_inc(bounds_made, 1)

            def digits(n, cols_i):
                nc.vector.tensor_scalar(digit_t[:, :], cols_i, P - 1, None, ALU.bitwise_and)
                ordered()
                nc.vector.tensor_copy(lo[n], digit_t[:, :])
                ordered()
                nc.vector.tensor_scalar(digit_t[:, :], cols_i, P.bit_length() - 1, None, ALU.arith_shift_right)
                ordered()
                nc.vector.tensor_copy(hi[n], digit_t[:, :])
                ordered()

            v.wait_ge(edges_in_cols, 1)
            digits(0, src_col[:, 0:TILES])
            for n, digit in enumerate((lo[0], hi[0])):
                last = nc.vector.tensor_scalar(step_digits[:, n, :], digit[:, TILES - STEP_TILES:TILES], 0.5, None,
                                               ALU.subtract)
            last.then_inc(step_digits_made, 1)
            v.wait_ge(consts_made, 17)
            hot_batch(0, 0, 0, 0)
            hot_batch(1, 1, 1, 0)
            with v.Fori(1, SRC_BATCHES // 2) as b:
                for half in range(2):
                    hot_batch(2 * b + half, 2 * b + half, half, 0)
            v.wait_ge(bounds_turned, 1)
            for n, to in enumerate((gmin, gmax)):
                from_tiles = banks[0:BLOCKS, n, 0:P].rearrange("b (j t) -> b j t", t=GT)
                last = nc.vector.tensor_reduce(to[:, :], from_tiles, AX.X, (ALU.min, ALU.max)[n])
            last.then_inc(bounds_read, 1)
            ordered()
            nc.vector.tensor_copy(gmin_i[:, :], gmin[:, :]).then_inc(bases_made, 1)
            v.wait_ge(steps_used, STEP_BATCHES + 3)
            nc.vector.tensor_copy(step_rows[0], step_sums)
            ordered()
            nc.vector.tensor_tensor(step_rows[1][:, 1:HI], step_sums[:, 1:HI], step_rows[0][:, 0:HI - 1], ALU.subtract)
            nc.vector.tensor_tensor(step_rows[1][:, 0:1], step_sums[:, 0:1], step_rows[0][:, HI - 1:HI],
                                    ALU.add).then_inc(step_diffs_made, 1)
            v.wait_ge(counts_whole, 1)
            nc.vector.tensor_scalar(r[:, :], hist, 1.0, None, ALU.max).then_inc(degree_ready, 1)
            v.wait_ge(degree_rooted, 1)
            nc.vector.reciprocal(r[:, :], root[:, :]).then_inc(r_made, 1)
            ordered()
            v.wait_ge(x_loaded, 32)
            for c, (first, end) in enumerate(X_CHUNKS):
                for w in range(first, end - (end - first) * 2 // 5):
                    nc.vector.tensor_scalar(x_all[:, w, :], x_all[:, w, :], r[:, w:w + 1], None, ALU.mult)
                ordered()
                v.wait_ge(x_scaled_act, c + 1)
                v.sem_inc(x_scaled, 1)
            nc.vector.tensor_copy(floor_f[:, :], floor_i[:, :])
            ordered()
            nc.vector.tensor_copy(floor_f[:, :].rearrange("b (i k) -> b i k", k=GR)[:, :, LAST_K + 1:],
                                  floor_late[:, :, :])
            ordered()
            nc.vector.tensor_tensor(gmax[:, :], gmax[:, :], gmin[:, :], ALU.subtract)
            nc.vector.tensor_scalar(floor_f[:, :], floor_f[:, :], float(PAD_DST), None, ALU.min)
            ordered()
            nc.vector.tensor_scalar(gmax[:, :], gmax[:, :], float(WIN - 1), None, ALU.is_gt)
            nc.vector.tensor_tensor(floor_f[:, :], gmin[:, :], floor_f[:, :], ALU.is_lt)
            ordered()
            nc.vector.tensor_tensor(gmax[:, :], gmax[:, :], floor_f[:, :], ALU.max)
            ordered()
            nc.vector.tensor_reduce(bad[:, 0:1], gmax[:, :], AX.X, ALU.max).then_inc(bad_counted, 1)
            v.wait_ge(bad_summed, 1)
            nc.vector.tensor_scalar(flag[:, :], banks[0:1, 2, 0:1], 0.0, None, ALU.is_gt).then_inc(flag_made, 1)
            v.wait_ge(bases_loaded, 16)
            nc.vector.tensor_copy(base_row_f[:, :], base_row[:, :]).then_inc(bases_float, 1)
            v.wait_ge(edges_in_cols, 2)
            nc.vector.tensor_copy(digit_t[:, :], dst_col[:, :])
            ordered()
            nc.vector.tensor_scalar(dst_rel[:, 0:TILES].bitcast(I32), digit_t[:, :], P.bit_length() - 1, None, ALU.arith_shift_right)
            ordered()
            nc.vector.tensor_copy(hi[1][:, 0:TILES], dst_rel[:, 0:TILES].bitcast(I32))
            ordered()
            nc.vector.tensor_scalar(dst_rel[:, 0:TILES].bitcast(I32), digit_t[:, :], P - 1, None, ALU.bitwise_and)
            ordered()
            nc.vector.tensor_copy(lo[1][:, 0:TILES], dst_rel[:, 0:TILES].bitcast(I32))
            ordered()
            v.wait_ge(bases_spread, 1)
            nc.vector.tensor_tensor(dst_rel[:, 0:TILES].rearrange("p (g t) -> p g t", t=GT),
                                    dst_col[:, :].rearrange("p (g t) -> p g t", t=GT),
                                    banks[:, 3, 0:GROUPS].unsqueeze(2).to_broadcast([P, GROUPS, GT]), ALU.subtract)
            ordered()
            nc.vector.tensor_copy(dst_rel[:, TILES:TILES + AHEAD * GT], dst_rel[:, 0:AHEAD * GT])
            ordered()

            def group_hot(first_tile, buf, raw=False):
                rel = dst_rel[:, bass.ds(first_tile, GT)].unsqueeze(2).to_broadcast([P, GT, WIN])
                last = nc.vector.tensor_tensor(dst_hot[:, buf, :, :],
                                               win_iota[:, :].unsqueeze(1).to_broadcast([P, GT, WIN]),
                                               rel, ALU.is_equal)
                if raw:
                    if first_tile == FIRST_GROUPS * GT:
                        v.wait_ge(r_edges_in[1], 16 * (len(RAW_LATE) - RAW_FIRST))
                    ordered()
                    scale = r_edge[:, first_tile:first_tile + GT].unsqueeze(2).to_broadcast([P, GT, WIN])
                    last = nc.vector.tensor_tensor(dst_hot[:, buf, :, :], dst_hot[:, buf, :, :], scale, ALU.mult)
                last.then_inc(dst_hot_made, 1)

            hot_batch(SRC_BATCHES, 0, 0, 1)
            nc.vector.memset(big[:, NW * D:KF * ACC_N], 0.0)
            for c, (first, end) in enumerate(X_CHUNKS):
                if c % 2 == 0:
                    v.wait_ge(table_stored[c], 16)
                    nc.vector.memset(big[:, first * D:end * D], 0.0)
            v.wait_ge(r_edges_in[0], 16 * (RAW_FIRST + len(RAW_EARLY)))
            for g in range(AHEAD):
                group_hot(g * GT, g, raw=True)

            def load_base(i, k):
                return v.value_load(base_row[0:1, bass.ds(i * GR + k, 1)], min_val=0, max_val=NPAD)

            def add_group(layer, i, k, base):
                v.wait_ge(tiles_done, group_no(layer, i, k) * GT + GT + U)
                here = acc[:, :, bass.ds(base, WIN)]
                nc.vector.tensor_tensor(here, group_sum(k % 2), here, ALU.add).then_inc(groups_added, 1)

            def diagonals(m):
                for s in range(2):
                    nc.vector.tensor_scalar(r_diag[s][:, :], ident[:, :], root[:, bass.ds(2 * m + s, 1)], None,
                                            ALU.mult).then_inc(diag_ready, 1)

            def mix(m, s, sums):
                v.wait_ge(x_turned, 2 * m + s + 1)
                nc.vector.tensor_tensor(xa[s][:, :, :], turned[s][:, 0, :, :], sums, ALU.mult)
                ordered()
                nc.vector.tensor_tensor(sum_a[s][:, :, :], turned[s][:, 1, :, :], sums, ALU.add).then_inc(mixed, 1)

            def finish_sums(layer, m):
                two = bass.ds(2 * m, 2)
                for s in range(2):
                    v.wait_ge(stored[s], 16 * (node_no(layer, m) + 1))
                if layer == 0:
                    nc.vector.scalar_tensor_tensor(pair[0], deg[:, two], 1.0, r[:, two], ALU.min, ALU.mult)
                    ordered()
                    for s in range(2):
                        v.wait_ge(projected, 2 * m + s + 1)
                        nc.vector.scalar_tensor_tensor(e[s][:, :], project[s], scal[:, s:s + 1], b0_s[:, :],
                                                       ALU.mult, ALU.add)
                    ordered()
                    for s in range(2):
                        nc.vector.scalar_tensor_tensor(e[s][:, :], e[s][:, :], 0.01, e[s][:, :], ALU.mult, ALU.max)
                    ordered()
                    for s in range(2):
                        nc.vector.tensor_tensor_reduce(out=out_t[s][:, :], in0=e[s][:, :], in1=e[s][:, :], scale=1.0,
                                                       scalar=0.0, op0=ALU.mult, op1=ALU.add,
                                                       accum_out=scal[:, 2 + s:3 + s])
                    ordered()
                    v.sem_inc(square_ready, 1)
                else:
                    nc.vector.tensor_scalar(pair[0], deg[:, two], 1.0, None, ALU.add)
                    ordered()
                    nc.vector.reciprocal(pair[1], pair[0])
                    ordered()
                    nc.vector.tensor_tensor(pair[2], pair[1], deg[:, two], ALU.mult)
                    ordered()
                    for s in range(2):
                        v.wait_ge(x_in[s], 16 * (node_no(1, m) + 1))
                        nc.vector.scalar_tensor_tensor(e[s][:, :], b1_s[:, :], scal[:, 4 + s:5 + s], x_t[s][:, :],
                                                       ALU.mult, ALU.add)
                    ordered()
                    for s in range(2):
                        v.wait_ge(projected, NW + 2 * m + s + 1)
                        nc.vector.scalar_tensor_tensor(out_t[s][:, :], project[s], scal[:, 2 + s:3 + s], e[s][:, :],
                                                       ALU.mult, ALU.add)
                    ordered()

            def moments(layer, m):
                if layer == 0:
                    v.wait_ge(norm_ready, m + 1)
                    nc.vector.tensor_scalar(pair[2], pair[2], 1e-12, None, ALU.max)
                    ordered()
                    nc.vector.reciprocal(pair[0], pair[2])
                    ordered()
                    for s in range(2):
                        nc.vector.scalar_tensor_tensor(out_t[s][:, :], e[s][:, :], scal[:, s:s + 1], x_t[s][:, :],
                                                       ALU.mult, ALU.add)
                    ordered()
                for s in range(2):
                    nc.vector.bn_stats(stats[:, s, :], out_t[s][:, :])
                ordered()
                for s in range(2):
                    nc.vector.bn_aggr(mv[:, s, :], stats[:, s, :])
                ordered()
                v.sem_inc(var_ready, 1)

            def norm(layer, m):
                v.wait_ge(var_rooted, node_no(layer, m) + 1)
                nc.vector.reciprocal(pair[3], pair[3])
                ordered()
                for s in range(2):
                    nc.vector.tensor_scalar(out_t[s][:, :], out_t[s][:, :], mv[:, s, 0:1], scal[:, 6 + s:7 + s],
                                            ALU.subtract, ALU.mult).then_inc(out_ready[s], 1)
                ordered()

            def add_hist(n):
                v.wait_ge(hot_used, n + 3)
                nc.vector.tensor_tensor(deg[:, :], hist, deg[:, :], ALU.add).then_inc(hist_added, 1)
                ordered()

            def round_(layer, i, finish):
                base = load_base(i, 0)
                for k in range(GR):
                    first_tile = i * U + (k + AHEAD) * GT
                    group_hot(first_tile, (k + AHEAD) % HOTS,
                              raw=layer == 0 and isinstance(i, int) and first_tile < RAW)
                    add_group(layer, i, k, base)
                    if k < GR - 1:
                        base = load_base(i, k + 1)
                    ordered()
                    if layer == 0 and k in (0, 3):
                        half = k // 3
                        hot_batch(SRC_BATCHES + 2 * i + half + 1, 2 * i + half + 1, 1 - half, 1)
                    if layer == 0 and k % 4 == 1:
                        add_hist(SRC_BATCHES + 2 * i + k // 4)
                    if finish and layer == 0 and k == LAST_K:
                        for s in range(2):
                            mix(i - 1, s, acc[:, :, bass.ds((2 * i - 2 + s) * P, P)])
                    if layer == 0 and k == LAST_K + 4:
                        diagonals(i)
                    if finish and LAST_K + 2 <= k <= LAST_K + 4:
                        (finish_sums, moments, norm)[k - LAST_K - 2](layer, i - 1)

            v.wait_ge(w_copied, 1)
            v.wait_ge(weights_loaded, 96)
            v.wait_ge(flag_made, 1)
            disordered = v.value_load(flag[0:1, 0:1], min_val=0, max_val=1)
            with v.If(disordered == 0):
                v.wait_ge(acc_zeroed_act, 1)
                ordered()
                for layer in range(2):
                    if layer == 1:
                        v.wait_ge(acc_zeroed, NW)
                    round_(layer, 0, False)
                    with v.Fori(1, ROUNDS) as i:
                        round_(layer, i, True)
                    if layer == 0:
                        for s in range(2):
                            mix(ROUNDS - 1, s, acc[:, :, (NW - 2 + s) * P:(NW - 1 + s) * P])
                    for step in (finish_sums, moments, norm):
                        step(layer, ROUNDS - 1)
            with v.Else():
                v.wait_ge(acc_zeroed_act, 1)
                ordered()
                v.sem_inc(acc_zeroed, 1)
                with v.Fori(0, HBATCHES // 2) as b:
                    for half in range(2):
                        hot_batch(SRC_BATCHES + 2 * b + half + 1, 2 * b + half + 1, 1 - half, 1)
                        add_hist(SRC_BATCHES + 2 * b + half)
                for layer in range(2):
                    with v.Fori(0, TILES) as t:
                        n = layer * TILES + t
                        v.wait_ge(tile_over, n + 1)
                        nc.vector.tensor_copy(scal[:, 5:6], dst_col[:, bass.ds(t, 1)]).then_inc(dcol_ready, 1)
                        ordered()
                        v.wait_ge(drow_spread, n + 1)
                        nc.vector.tensor_scalar(same(ring), banks[:, 0, 0:P], scal[:, 5:6], None,
                                                ALU.is_equal).then_inc(same_ready, 1)
                        ordered()
                        nc.vector.tensor_tensor_reduce(out=ring[:, 3, 0:P], in0=same(ring), in1=lower[:, :], scale=1.0,
                                                       scalar=0.0, op0=ALU.mult, op1=ALU.add, accum_out=scal[:, 6:7])
                        ordered()
                        nc.vector.tensor_scalar(scal[:, 6:7], scal[:, 6:7], 0.0, None, ALU.is_equal)
                        nc.vector.tensor_tensor(scal[:, 7:8], scal[:, 5:6], dump_row[:, :], ALU.subtract)
                        ordered()
                        nc.vector.scalar_tensor_tensor(scal[:, 7:8], scal[:, 7:8], scal[:, 6:7], dump_row[:, :],
                                                       ALU.mult, ALU.add)
                        ordered()
                        nc.vector.tensor_copy(idx[:, 1:2], scal[:, 7:8])
                        v.wait_ge(combined, n + 1)
                        nc.vector.tensor_copy(ring[:, 1, :], banks[:, 1, 0:D])
                        ordered()
                        v.sem_inc(comb_ready, 1)
                    with v.Fori(0, ROUNDS) as m:
                        for s in range(2):
                            if layer == 0:
                                if s == 0:
                                    diagonals(m)
                                v.wait_ge(a_ready[s], m + 1)
                                mix(m, s, a_t[s][:, :, :])
                        for step in (finish_sums, moments, norm):
                            step(layer, m)

        @block.tensor
        def _(pe):
            pe.sem_inc(hot_used, 2)
            pe.sem_inc(steps_used, 3)
            pe.sem_inc(tiles_done, U)
            pe.wait_ge(consts_made, 17)

            def turn_edges(n):
                pe.wait_ge(edges_float, n + 1)
                for b in range(BLOCKS):
                    rows = P if b < BLOCKS - 1 else LAST_BLOCK_TILES
                    last = nc.tensor.transpose(banks[:, 4 * n + b // 4, (b % 4) * P:(b % 4) * P + rows],
                                               nat[n][0:rows, b * P:(b + 1) * P], ident[0:rows, 0:rows])
                last.then_inc(edges_turned, 1)

            def hist_batch(n, half, first, last_one):
                pe.wait_ge(hot_made, n + 1)
                for t in range(HB):
                    last = nc.tensor.matmul(hist, lo_hot[half][:, :, t], hi_hot[half][:, :, t],
                                            start=first and t == 0, stop=last_one and t == HB - 1)
                last.then_inc(hot_used, 1)

            def step_batch(n, third, first, last_one):
                pe.wait_ge(steps_made, n + 1)
                for t in range(SB):
                    last = nc.tensor.matmul(step_sums, steps[:, third, t, 0:P], steps[:, third, t, P:P + HI],
                                            start=first and t == 0, stop=last_one and t == SB - 1)
                last.then_inc(steps_used, 1)

            turn_edges(0)
            turn_edges(1)
            pe.wait_ge(bounds_made, 1)
            pe.wait_ge(edges_in_cols, 1)
            for n in range(2):
                last = nc.tensor.transpose(banks[0:BLOCKS, n, 0:P], bounds[:, n, :], ident[:, :])
            last.then_inc(bounds_turned, 1)
            pe.wait_ge(edges_in_cols, 2)
            def span(n, first, last_one):
                per_span, steps_per_span = SRC_BATCHES // SPANS, STEP_BATCHES // SPANS
                for k in range(per_span):
                    hist_batch(n * per_span + k, k % 2, first and k == 0, False)
                    if k < steps_per_span:
                        step_batch(n * steps_per_span + k, k % 3, first and k == 0,
                                   last_one and k == steps_per_span - 1)

            span(0, True, False)
            with pe.Fori(1, SPANS - 1) as n:
                span(n, False, False)
            span(SPANS - 1, False, True)
            pe.wait_ge(step_diffs_made, 1)
            nc.tensor.matmul(hist, between[:, :], step_rows[1], start=False, stop=True).then_inc(counts_whole, 1)
            pe.wait_ge(bounds_read, 1)
            pe.wait_ge(r_made, 1)
            nc.tensor.transpose(banks[0:NW, 2, 0:P], r[:, :], ident[:, :]).then_inc(r_turned, 1)
            pe.wait_ge(weights_loaded, 96)
            for o, half in enumerate(xa):
                for k in range(KF):
                    last = nc.tensor.transpose(banks[:, 0, k * D + o * P:k * D + (o + 1) * P], half[:, k, :], ident[:, :])
            last.then_inc(w_turned, 1)
            pe.wait_ge(r_rows_made, 1)
            pe.wait_ge(bad_counted, 1)
            nc.tensor.matmul(banks[0:1, 2, 0:1], bad[:, 0:1], ones[0:BLOCKS, 0:1],
                             start=True, stop=True).then_inc(bad_summed, 1)
            pe.wait_ge(bases_float, 1)
            nc.tensor.matmul(banks[:, 3, 0:GROUPS], ones[0:1, :], base_row_f[:, 0:GROUPS],
                             start=True, stop=True).then_inc(bases_spread, 1)

            def turn_x(m, s):
                if s == 0:
                    pe.wait_ge(diag_ready, 2 * m + 2)
                pe.wait_ge(x_in[s], 16 * (m + 1))
                for k in range(KF):
                    nc.tensor.transpose(turned[s][:, 0, k, :], x_t[s][:, k * P:(k + 1) * P], ident[:, :])
                for k in range(KF):
                    last = nc.tensor.matmul(turned[s][:, 1, k, :], x_t[s][:, k * P:(k + 1) * P], r_diag[s][:, :],
                                            start=True, stop=True)
                last.then_inc(x_turned, 1)

            def products(layer, m, s, taken):
                if layer == 0:
                    pe.wait_ge(mixed, 2 * m + 2 if s == 1 else 2 * m + 1)
                    parts = [(xa[s][:, k, :], w2_s[:, k, :]) for k in range(KF)]
                    parts += [(sum_a[s][:, k, :], w1_s[:, k, :]) for k in range(KF)]
                else:
                    pe.wait_ge(a_ready[s], taken + 1)
                    parts = [(a_t[s][:, k, :], wt_s[:, k, :]) for k in range(KF)]
                for k, (left, right) in enumerate(parts):
                    last = nc.tensor.matmul(project[s], left, right, start=k == 0, stop=k == len(parts) - 1)
                last.then_inc(projected, 1)

            def dst_hist(n, half):
                pe.wait_ge(hist_added, n - SRC_BATCHES + 1)
                hist_batch(n, half, True, True)

            def round_(layer, i, finish, end=U):
                for k in range(GR):
                    if layer == 0 and k in (0, GR // 2):
                        half = k // (GR // 2)
                        dst_hist(SRC_BATCHES + 2 * i + half, half)
                    pe.wait_ge(dst_hot_made, group_no(layer, i, k) + 1)
                    pe.wait_ge(groups_added, group_no(layer, i, k) + 1)
                    for j in range(GT):
                        u = k * GT + j
                        if u < end:
                            rounds_before = layer * (ROUNDS if u < FINAL else ROUNDS - 1) + i
                            pe.wait_ge(rows_in[u], 16 * (rounds_before + 1))
                        for f in range(KF):
                            last = nc.tensor.matmul(group_sum(k % 2)[:, f, :], ring[:, u, f * P:(f + 1) * P],
                                                    dst_hot[:, k % HOTS, j, :], start=j == 0, stop=j == GT - 1)
                        last.then_inc(tiles_done, 1)
                    if finish and layer == 0 and k == LAST_K:
                        for s in range(2):
                            turn_x(i - 1, s)
                    if finish and k == LAST_K + 1:
                        for s in range(2):
                            products(layer, i - 1, s, i - 1)

            pe.wait_ge(r_made, 1)
            pe.wait_ge(w_copied, 1)
            pe.wait_ge(flag_made, 1)
            disordered = pe.value_load(flag[0:1, 0:1], min_val=0, max_val=1)
            with pe.If(disordered == 0):
                for layer in range(2):
                    round_(layer, 0, False)
                    with pe.Fori(1, ROUNDS - 1) as i:
                        round_(layer, i, True)
                    round_(layer, ROUNDS - 1, True, FINAL)
                    if layer == 0:
                        for s in range(2):
                            turn_x(ROUNDS - 1, s)
                    for s in range(2):
                        products(layer, ROUNDS - 1, s, ROUNDS - 1)
            with pe.Else():
                with pe.Fori(0, HBATCHES // 2) as b:
                    for half in range(2):
                        dst_hist(SRC_BATCHES + 2 * b + half, half)
                for layer in range(2):
                    with pe.Fori(0, TILES) as t:
                        n = layer * TILES + t
                        pe.wait_ge(dcol_ready, n + 1)
                        nc.tensor.matmul(banks[:, 0, 0:P], scal[:, 5:6].to_broadcast([P, P]), ident[:, :],
                                         start=True, stop=True).then_inc(drow_spread, 1)
                        pe.wait_ge(same_ready, n + 1)
                        pe.wait_ge(row_in, 16 * (n + 1))
                        nc.tensor.matmul(banks[:, 1, 0:D], same(ring), ring[:, 0, :],
                                         start=True, stop=True).then_inc(combined, 1)
                    with pe.Fori(0, ROUNDS) as m:
                        for s in range(2):
                            pe.wait_ge(sums_in, 16 * (layer * NW + 2 * m + s + 1))
                            for k in range(KF):
                                last = nc.tensor.transpose(banks[:, 0, k * P:(k + 1) * P],
                                                           sums_t[:, k * P:(k + 1) * P], ident[:, :])
                            last.then_inc(sums_turned, 1)
                            if layer == 0:
                                turn_x(m, s)
                            products(layer, m, s, node_no(layer, m))


def same(ring):
    return ring[:, 2, 0:P]


_INS = ["x", "src", "dst", "L0_gnn_W1", "L0_gnn_W2", "L0_gnn_b", "L1_gnn_W", "L1_gnn_b"]


def kernel(**inputs):
    import numpy as np
    import concourse.bacc as bacc
    from concourse import mybir as mb
    from concourse.bass_utils import run_bass_kernel_spmd

    nc = bacc.Bacc("TRN2", target_bir_lowering=False, num_devices=1)
    arrays, args = {}, []
    for name in _INS:
        a = np.ascontiguousarray(inputs[name])
        arrays[f"in_{name}"] = a
        args.append(nc.dram_tensor(f"in_{name}", a.shape, mb.dt.from_np(a.dtype), kind="ExternalInput").ap())
    result = nc.dram_tensor("result", (NODES, D), mb.dt.float32, kind="ExternalOutput").ap()
    gnn(nc, *args, result)
    r = run_bass_kernel_spmd(nc, [arrays], core_ids=[0])
    return r.results[0]["result"]
```
